# Optimizing a Trainium2 kernel written in Bass

```python
import numpy as np
import jax
import jax.numpy as jnp

def _softmax(x, axis=-1):
    return jax.nn.softmax(x, axis=axis)

def _gelu(x):
    return jax.nn.gelu(x, approximate=True)

def _silu(x):
    return jax.nn.silu(x)

def _sigmoid(x):
    return jax.nn.sigmoid(x)

def _layernorm(x, axis=-1, eps=1e-05):
    m = jnp.mean(x, axis=axis, keepdims=True)
    v = jnp.var(x, axis=axis, keepdims=True)
    return (x - m) / jnp.sqrt(v + eps)

def _scatter_add(tgt, idx, src, axis=0):
    return tgt.at[idx].add(src)

def _segment_sum(src, seg, n):
    return jax.ops.segment_sum(src, seg, n)
kernel_name = 'mk_gnn_resnorm_d4_gnn_r8_bea325'

def setup_inputs(seed: int=0):
    np.random.seed(seed)
    _w = jnp.asarray

    def _rec_inputs():
        import jax
        import jax.numpy as jnp
        _gk = jax.random.key(seed)
        x = -0.0005121 + 1.001 * jax.random.normal(jax.random.fold_in(_gk, 1), (12500, 64), jnp.float32)
        src = jax.random.randint(jax.random.fold_in(_gk, 2), (400000,), 0, 12500, jnp.int32)
        dst = jax.random.randint(jax.random.fold_in(_gk, 3), (400000,), 0, 12500, jnp.int32)
        _o = jnp.argsort(dst, stable=True)
        src = src[_o]
        dst = dst[_o]
        edge_type_64 = jax.random.randint(jax.random.fold_in(_gk, 13), (400000,), 0, 64, jnp.int32)
        edge_weight1 = jax.random.uniform(jax.random.fold_in(_gk, 14), (400000, 1), jnp.float32, 0.0, 0.999998)
        return (x, src, dst, edge_type_64, edge_weight1)
    x, src, dst, edge_type_64, edge_weight1 = _rec_inputs()

    def _L0_gnn_setup():
        import jax, jax.numpy as jnp
        import numpy as np
        N, E, D = (6250, 100000, 64)
        key = jax.random.key(seed)
        ks = jax.random.split(key, 8)
        s = 1.0 / np.sqrt(2 * D)
        inp = {'node_emb': jax.random.normal(ks[0], (N, D), dtype=jnp.float32), 'edge_index': jax.random.randint(ks[1], (2, E), 0, N, dtype=jnp.int64), 'W1': jax.random.normal(ks[2], (2 * D, D), dtype=jnp.float32) * s, 'b1': jnp.zeros((D,), dtype=jnp.float32), 'W2': jax.random.normal(ks[3], (D, D), dtype=jnp.float32) * (1.0 / np.sqrt(D)), 'b2': jnp.zeros((D,), dtype=jnp.float32), 'Wg': jax.random.normal(ks[4], (D, D), dtype=jnp.float32) * (1.0 / np.sqrt(D)), 'bg': jnp.zeros((D,), dtype=jnp.float32)}
        return inp
    _L0_gnn_all = _L0_gnn_setup()
    _L0_gnn_in = {k: v for k, v in _L0_gnn_all.items() if k in ('W1', 'b1', 'W2', 'b2', 'Wg', 'bg')}
    del _L0_gnn_all

    def _L1_gnn_setup():
        import jax, jax.numpy as jnp
        import numpy as np
        N_NODES = 12500
        N_EDGES = 160000
        D = 64
        key = jax.random.key(seed)
        k1, k2, k3, k4, k5, k6 = jax.random.split(key, 6)
        feat = jax.random.normal(k1, (N_NODES, D), dtype=jnp.float32)
        W_attn = jax.random.normal(k2, (D, 2 * D), dtype=jnp.float32) * 0.1
        b_attn = jax.random.normal(k3, (D,), dtype=jnp.float32) * 0.1
        w_out = jax.random.normal(k4, (D,), dtype=jnp.float32) * 0.1
        src = jax.random.randint(k5, (N_EDGES,), 0, N_NODES, dtype=jnp.int32)
        dst = jax.random.randint(k6, (N_EDGES,), 0, N_NODES, dtype=jnp.int32)
        return {'feat': feat, 'W_attn': W_attn, 'b_attn': b_attn, 'w_out': w_out, 'src': src, 'dst': dst}
    _L1_gnn_all = _L1_gnn_setup()
    _L1_gnn_in = {k: v for k, v in _L1_gnn_all.items() if k in ('W_attn', 'b_attn', 'w_out')}
    del _L1_gnn_all

    def _L2_gnn_setup():
        import jax, jax.numpy as jnp
        import numpy as np
        N_NODES = 12500
        N_EDGES = 200000
        NHID = 64
        NFEAT = 64
        BN_EPS = 1e-05
        NEG_SLOPE = 0.2

        def gat_conv(x, W, a_src_w, a_dst_w, b, src, dst, n):
            h = x @ W
            a_src = h @ a_src_w
            a_dst = h @ a_dst_w
            e = jax.nn.leaky_relu(a_src[src] + a_dst[dst], NEG_SLOPE)
            m = jax.ops.segment_max(e, dst, num_segments=n)
            m = jnp.where(jnp.isfinite(m), m, 0.0)
            w = jnp.exp(e - m[dst])
            s = jax.ops.segment_sum(w, dst, num_segments=n)
            alpha = w / (s[dst] + 1e-16)
            out = jax.ops.segment_sum(alpha[:, None] * h[src], dst, num_segments=n)
            return out + b
        key = jax.random.key(seed)
        ks = jax.random.split(key, 12)
        s = 0.1
        return {'x': jax.random.normal(ks[0], (N_NODES, NHID), jnp.float32), 'adj': jax.random.randint(ks[1], (2, N_EDGES), 0, N_NODES, jnp.int32), 'W1': jax.random.normal(ks[2], (NHID, NHID), jnp.float32) * s, 'as1': jax.random.normal(ks[3], (NHID,), jnp.float32) * s, 'ad1': jax.random.normal(ks[4], (NHID,), jnp.float32) * s, 'b1': jax.random.normal(ks[5], (NHID,), jnp.float32) * s, 'bn_gamma': jnp.ones((NHID,), jnp.float32), 'bn_beta': jnp.zeros((NHID,), jnp.float32), 'bn_mean': jnp.zeros((NHID,), jnp.float32), 'bn_var': jnp.ones((NHID,), jnp.float32), 'W2': jax.random.normal(ks[6], (NHID, NFEAT), jnp.float32) * s, 'as2': jax.random.normal(ks[7], (NFEAT,), jnp.float32) * s, 'ad2': jax.random.normal(ks[8], (NFEAT,), jnp.float32) * s, 'b2': jax.random.normal(ks[9], (NFEAT,), jnp.float32) * s}
    _L2_gnn_all = _L2_gnn_setup()
    _L2_gnn_in = {k: v for k, v in _L2_gnn_all.items() if k in ('W1', 'as1', 'ad1', 'b1', 'bn_gamma', 'bn_beta', 'bn_mean', 'bn_var', 'W2', 'as2', 'ad2', 'b2')}
    del _L2_gnn_all

    def _L3_gnn_setup():
        import jax, jax.numpy as jnp
        import numpy as np
        N_NODES = 6250
        N_EDGES = 200000
        IN_F = 64
        OUT_F = 64
        NUM_RELS = 64
        NUM_BASES = 64
        BN_EPS = 1e-05
        key = jax.random.key(seed)
        ks = jax.random.split(key, 12)
        node_feats = jax.random.normal(ks[0], (N_NODES, IN_F), dtype=jnp.float32)
        src = jax.random.randint(ks[1], (N_EDGES,), 0, N_NODES, dtype=jnp.int32)
        dst = jax.random.randint(ks[2], (N_EDGES,), 0, N_NODES, dtype=jnp.int32)
        etype = jax.random.randint(ks[3], (N_EDGES,), 0, NUM_RELS, dtype=jnp.int32)
        norm = jax.random.uniform(ks[4], (N_EDGES, 1), dtype=jnp.float32)
        basis = jax.random.normal(ks[5], (NUM_BASES, IN_F, OUT_F), dtype=jnp.float32) * (1.0 / np.sqrt(IN_F))
        comp = jax.random.normal(ks[6], (NUM_RELS, NUM_BASES), dtype=jnp.float32) * (1.0 / np.sqrt(NUM_BASES))
        bias = jnp.zeros((OUT_F,), dtype=jnp.float32)
        res_w = jax.random.normal(ks[7], (OUT_F, IN_F), dtype=jnp.float32) * (1.0 / np.sqrt(IN_F))
        res_b = jnp.zeros((OUT_F,), dtype=jnp.float32)
        gamma = jnp.ones((OUT_F,), dtype=jnp.float32)
        beta = jnp.zeros((OUT_F,), dtype=jnp.float32)
        return {'node_feats': node_feats, 'src': src, 'dst': dst, 'etype': etype, 'norm': norm, 'basis': basis, 'comp': comp, 'bias': bias, 'res_w': res_w, 'res_b': res_b, 'gamma': gamma, 'beta': beta}
    _L3_gnn_all = _L3_gnn_setup()
    _L3_gnn_in = {k: v for k, v in _L3_gnn_all.items() if k in ('basis', 'comp', 'bias', 'res_w', 'res_b', 'gamma', 'beta')}
    del _L3_gnn_all
    return {'x': x, 'src': src, 'dst': dst, 'edge_type_64': edge_type_64, 'edge_weight1': edge_weight1, 'L0_gnn_W1': _L0_gnn_in['W1'], 'L0_gnn_b1': _L0_gnn_in['b1'], 'L0_gnn_W2': _L0_gnn_in['W2'], 'L0_gnn_b2': _L0_gnn_in['b2'], 'L0_gnn_Wg': _L0_gnn_in['Wg'], 'L0_gnn_bg': _L0_gnn_in['bg'], 'L1_gnn_W_attn': _L1_gnn_in['W_attn'], 'L1_gnn_b_attn': _L1_gnn_in['b_attn'], 'L1_gnn_w_out': _L1_gnn_in['w_out'], 'L2_gnn_W1': _L2_gnn_in['W1'], 'L2_gnn_as1': _L2_gnn_in['as1'], 'L2_gnn_ad1': _L2_gnn_in['ad1'], 'L2_gnn_b1': _L2_gnn_in['b1'], 'L2_gnn_bn_gamma': _L2_gnn_in['bn_gamma'], 'L2_gnn_bn_beta': _L2_gnn_in['bn_beta'], 'L2_gnn_bn_mean': _L2_gnn_in['bn_mean'], 'L2_gnn_bn_var': _L2_gnn_in['bn_var'], 'L2_gnn_W2': _L2_gnn_in['W2'], 'L2_gnn_as2': _L2_gnn_in['as2'], 'L2_gnn_ad2': _L2_gnn_in['ad2'], 'L2_gnn_b2': _L2_gnn_in['b2'], 'L3_gnn_basis': _L3_gnn_in['basis'], 'L3_gnn_comp': _L3_gnn_in['comp'], 'L3_gnn_bias': _L3_gnn_in['bias'], 'L3_gnn_res_w': _L3_gnn_in['res_w'], 'L3_gnn_res_b': _L3_gnn_in['res_b'], 'L3_gnn_gamma': _L3_gnn_in['gamma'], 'L3_gnn_beta': _L3_gnn_in['beta']}

def reference(x, src, dst, edge_type_64, edge_weight1, L0_gnn_W1, L0_gnn_b1, L0_gnn_W2, L0_gnn_b2, L0_gnn_Wg, L0_gnn_bg, L1_gnn_W_attn, L1_gnn_b_attn, L1_gnn_w_out, L2_gnn_W1, L2_gnn_as1, L2_gnn_ad1, L2_gnn_b1, L2_gnn_bn_gamma, L2_gnn_bn_beta, L2_gnn_bn_mean, L2_gnn_bn_var, L2_gnn_W2, L2_gnn_as2, L2_gnn_ad2, L2_gnn_b2, L3_gnn_basis, L3_gnn_comp, L3_gnn_bias, L3_gnn_res_w, L3_gnn_res_b, L3_gnn_gamma, L3_gnn_beta):
    import jax
    import jax.numpy as jnp

    def _L0_gnn_ref(node_emb, edge_index, W1, b1, W2, b2, Wg, bg):
        import jax, jax.numpy as jnp
        import numpy as np
        src, dst = (edge_index[0], edge_index[1])
        pair_emb = jnp.concatenate([node_emb[src], node_emb[dst]], axis=-1)
        h = jax.nn.relu(pair_emb @ W1 + b1)
        interaction = h @ W2 + b2
        gate = jax.nn.sigmoid(interaction @ Wg + bg)
        gated = interaction * gate
        N = node_emb.shape[0]
        summed = jax.ops.segment_sum(gated, src, num_segments=N)
        counts = jax.ops.segment_sum(jnp.ones((src.shape[0],), dtype=gated.dtype), src, num_segments=N)
        pooled = summed / jnp.maximum(counts, 1.0)[:, None]
        return pooled

    def _L1_gnn_ref(feat, W_attn, b_attn, w_out, src, dst):
        import jax, jax.numpy as jnp
        import numpy as np
        N_NODES = 12500
        N_EDGES = 160000
        D = 64
        N = feat.shape[0]
        h_src = feat[src]
        h_dst = feat[dst]
        hc = jnp.concatenate([h_src, h_dst], axis=-1)
        hc = jnp.tanh(hc @ W_attn.T + b_attn)
        e = hc @ w_out
        m = jax.ops.segment_max(e, dst, num_segments=N)
        m = jnp.where(jnp.isfinite(m), m, 0.0)
        ex = jnp.exp(e - m[dst])
        denom = jax.ops.segment_sum(ex, dst, num_segments=N)
        alpha = ex / jnp.where(denom == 0.0, 1.0, denom)[dst]
        z = jax.ops.segment_sum(alpha[:, None] * h_src, dst, num_segments=N)
        return z

    def _L2_gnn_ref(x, adj, W1, as1, ad1, b1, bn_gamma, bn_beta, bn_mean, bn_var, W2, as2, ad2, b2):
        import jax, jax.numpy as jnp
        import numpy as np
        N_NODES = 12500
        N_EDGES = 200000
        NHID = 64
        NFEAT = 64
        BN_EPS = 1e-05
        NEG_SLOPE = 0.2

        def gat_conv(x, W, a_src_w, a_dst_w, b, src, dst, n):
            h = x @ W
            a_src = h @ a_src_w
            a_dst = h @ a_dst_w
            e = jax.nn.leaky_relu(a_src[src] + a_dst[dst], NEG_SLOPE)
            m = jax.ops.segment_max(e, dst, num_segments=n)
            m = jnp.where(jnp.isfinite(m), m, 0.0)
            w = jnp.exp(e - m[dst])
            s = jax.ops.segment_sum(w, dst, num_segments=n)
            alpha = w / (s[dst] + 1e-16)
            out = jax.ops.segment_sum(alpha[:, None] * h[src], dst, num_segments=n)
            return out + b
        n = x.shape[0]
        loops = jnp.arange(n, dtype=adj.dtype)
        src = jnp.concatenate([adj[0], loops])
        dst = jnp.concatenate([adj[1], loops])
        h = jax.nn.relu(gat_conv(x, W1, as1, ad1, b1, src, dst, n))
        h = (h - bn_mean) * jax.lax.rsqrt(bn_var + BN_EPS) * bn_gamma + bn_beta
        out = jax.nn.relu(gat_conv(h, W2, as2, ad2, b2, src, dst, n))
        return out

    def _L3_gnn_ref(node_feats, src, dst, etype, norm, basis, comp, bias, res_w, res_b, gamma, beta):
        import jax, jax.numpy as jnp
        import numpy as np
        N_NODES = 6250
        N_EDGES = 200000
        IN_F = 64
        OUT_F = 64
        NUM_RELS = 64
        NUM_BASES = 64
        BN_EPS = 1e-05
        N = node_feats.shape[0]
        R = comp.shape[0]
        W = jnp.einsum('rb,bio->rio', comp, basis)
        msg = node_feats[src] * norm
        seg = etype.astype(jnp.int32) * N + dst
        s = jax.ops.segment_sum(msg, seg, num_segments=R * N)
        s = s.reshape(R, N, -1)
        h = jnp.einsum('rni,rio->no', s, W) + bias
        h = jax.nn.relu(h)
        res = jax.nn.relu(node_feats @ res_w.T + res_b)
        y = h + res
        mean = jnp.mean(y, axis=0)
        var = jnp.var(y, axis=0)
        return (y - mean) * jax.lax.rsqrt(var + BN_EPS) * gamma + beta
    edge_index = jnp.stack([src, dst])
    x = _layernorm(x + _L0_gnn_ref(x, edge_index, L0_gnn_W1, L0_gnn_b1, L0_gnn_W2, L0_gnn_b2, L0_gnn_Wg, L0_gnn_bg), axis=-1)
    x = _layernorm(x + _L1_gnn_ref(x, L1_gnn_W_attn, L1_gnn_b_attn, L1_gnn_w_out, src, dst), axis=-1)
    x = _layernorm(x + _L2_gnn_ref(x, edge_index, L2_gnn_W1, L2_gnn_as1, L2_gnn_ad1, L2_gnn_b1, L2_gnn_bn_gamma, L2_gnn_bn_beta, L2_gnn_bn_mean, L2_gnn_bn_var, L2_gnn_W2, L2_gnn_as2, L2_gnn_ad2, L2_gnn_b2), axis=-1)
    x = _layernorm(x + _L3_gnn_ref(x, src, dst, edge_type_64, edge_weight1, L3_gnn_basis, L3_gnn_comp, L3_gnn_bias, L3_gnn_res_w, L3_gnn_res_b, L3_gnn_gamma, L3_gnn_beta), axis=-1)
    return x

_drawn_inputs = setup_inputs


def setup_inputs(seed=0):
    import zlib

    import numpy as np

    out = dict(_drawn_inputs(seed))
    spreads = {'L0_gnn_b1': (0.0, 0.1),
     'L0_gnn_b2': (0.0, 0.1),
     'L0_gnn_bg': (0.0, 0.393),
     'L2_gnn_bn_gamma': (1.0, 0.6),
     'L2_gnn_bn_beta': (0.0, 0.1),
     'L2_gnn_bn_mean': (0.0, 0.1),
     'L2_gnn_bn_var': (1.0, 0.6),
     'L3_gnn_bias': (0.0, 0.633),
     'L3_gnn_res_b': (0.0, 0.43),
     'L3_gnn_gamma': (1.0, 0.2),
     'L3_gnn_beta': (0.0, 0.1)}
    factors = {'L1_gnn_b_attn': 8.0,
     'L2_gnn_ad1': 42.44,
     'L2_gnn_as2': 41.982,
     'L2_gnn_ad2': 64.0,
     'L2_gnn_as1': 3.828}
    for name, (base, spread) in spreads.items():
        noise = np.random.default_rng([zlib.crc32(name.encode()), seed]).standard_normal(out[name].shape)
        drawn = base * np.exp(spread * noise) if base else spread * noise
        out[name] = jnp.asarray(drawn.astype(out[name].dtype))
    for name, factor in factors.items():
        out[name] = (out[name] * factor).astype(out[name].dtype)
    return out
```

```python
from contextlib import ExitStack, contextmanager

import concourse.bass as bass
from concourse import mybir

F32 = mybir.dt.float32
I32 = mybir.dt.int32
ALU = mybir.AluOpType
ACT = mybir.ActivationFunctionType
AX = mybir.AxisListType.X

P = 128
N = 12500
E = 400000
D = 64
R = 64
K = -(-N // P)
NP = P * K
L = E // P
T = 25
CH = L // T
RING = 3
LAG = 2
HEAD = 5
BIG = 1e30
SKIP = 1000000.0
NSMP = L // T
GRP = 4
GROUPS = [(g, min(GRP, T - g)) for g in range(0, T, GRP)]
NG = len(GROUPS)
ACCS = 5
OUTER = (CH - HEAD) // RING
ROW = D + 2
LN_EPS = 1e-5
BN_EPS = 1e-5
NEG_SLOPE = 0.2


def chunk_loop(eng, body):
    for j in range(HEAD):
        body(j, j % RING, j // RING)
    with eng.Fori(0, OUTER) as i:
        for v in range(RING):
            j = HEAD + v
            body(i * RING + j, j % RING, i + j // RING)


def since(j, first):
    return not isinstance(j, int) or j >= first


class Steps:

    def __init__(self, eng, sem):
        self.eng, self.sem, self.base, self.j, self.per, self.k = eng, sem, 0, None, 0, 0

    def chunk(self, j, per):
        if self.j is None:
            self.base += self.k
        self.j, self.per, self.k = j, per, 0

    def end_chunk(self):
        assert self.k == self.per, (self.k, self.per)

    def end_loop(self, chunks):
        self.base, self.j, self.k = self.base + chunks * self.per, None, 0

    def __call__(self, ins):
        self.k += 1
        ins.then_inc(self.sem, 1)
        value = self.base + self.k if self.j is None else self.j * self.per + (self.base + self.k)
        self.eng.wait_ge(self.sem, value)


def hold(eng, sem, value):
    eng.wait_ge(sem, value)
    eng.nop(nofuse=True)


def bc(ap, axis, shape):
    return ap.unsqueeze(axis).to_broadcast(shape)


def program(nc, x, src, dst, ety, ew, W, out):
    dram = lambda name, shape, dt=F32: nc.dram_tensor(name, shape, dt, kind="Internal").ap()
    start_d = dram("start_d", [NP, 1])
    last_d = dram("last_d", [NP, 1], I32)
    smp_d = dram("smp_d", [P, NSMP])
    idx3_d = dram("idx3_d", [P, L], I32)
    tabA_d = dram("tabA_d", [NP, D])
    tabB_d = dram("tabB_d", [NP, D])
    firstrows_d = dram("firstrows_d", [E, D])
    firstad_d = dram("firstad_d", [E, 1])
    tabG_d = dram("tabG_d", [NP, ROW + D])
    tabH_d = dram("tabH_d", [NP, ROW])
    tabS_d = dram("tabS_d", [NP, 1])
    state_d = dram("state_d", [E, ROW])
    wr_d = dram("wr_d", [R, D * D])
    y_d = dram("y_d", [NP * R, D])
    acc_d = [dram(f"acc{a}_d", [NP + P, D + 1]) for a in range(ACCS)]

    src_c = src.rearrange("(p l) -> p l", p=P)
    dst_c = dst.rearrange("(p l) -> p l", p=P)
    ety_c = ety.rearrange("(p l) -> p l", p=P)
    nodes = lambda ap: ap.rearrange("(p k) f -> p (k f)", k=K)

    ctx = ExitStack()
    with ctx:
        ctx.enter_context(nc.allow_non_contiguous_dma(reason="columns of one element per partition"))

        def sb(c, name, shape, dt=F32):
            return c.enter_context(nc.sbuf_tensor(name, shape, dt))

        scopes = []

        @contextmanager
        def phase():
            with ExitStack() as c:
                scopes.append([])
                yield c
            used = scopes.pop()
            if used:
                nc.clear_and_free_semaphores(used)
                nc.all_engine_barrier()

        def sem(name):
            scopes[-1].append(nc.alloc_semaphore(name))
            return scopes[-1][-1]

        def pool_dma_sem(name):
            return ctx.enter_context(nc.semaphore(name))

        bank = [ctx.enter_context(nc.psum_tensor(f"bank{i}", [P, 512], F32)) for i in range(8)]
        x_sb = sb(ctx, "x_sb", [P, K, D])
        ident = sb(ctx, "ident", [P, P])
        below = sb(ctx, "below", [P, P])
        above = sb(ctx, "above", [P, P])
        ones = sb(ctx, "ones", [P, P])
        cont = sb(ctx, "cont", [P, L])
        nonempty = sb(ctx, "nonempty", [P, K])
        last_i = sb(ctx, "last_i", [P, K], I32)
        first_i = sb(ctx, "first_i", [P, K], I32)
        head_i = sb(ctx, "head_i", [P, 1], I32)
        fix_i = sb(ctx, "fix_i", [P, 1], I32)
        lastq_i = sb(ctx, "lastq_i", [P, 1], I32)
        carryT = sb(ctx, "carryT", [P, P])
        trash = sb(ctx, "trash", [P, 1])
        real = sb(ctx, "real", [P, K])
        acc_landed = [pool_dma_sem(f"acc_landed{a}") for a in range(ACCS)]

        with phase() as c:
            dst_i = sb(c, "dst_i", [P, L], I32)
            dstf = sb(c, "dstf", [P, L])
            prev0_i = sb(c, "prev0_i", [P, 1], I32)
            prev0 = sb(c, "prev0", [P, 1])
            src_i = sb(c, "src_i", [P, L], I32)
            ety_i = sb(c, "ety_i", [P, L], I32)
            zeros = sb(c, "zeros", [P, 6435])
            nid_i = sb(c, "nid_i", [P, K], I32)
            nid = sb(c, "nid", [P, K])
            big = sb(c, "big", [P, K * P])
            smp = sb(c, "smp", [P, NSMP])
            frow = sb(c, "frow", [P, P])
            cnt = sb(c, "cnt", [P, K])
            blk = sb(c, "blk", [P, K])
            blk_i = sb(c, "blk_i", [P, K], I32)
            start = sb(c, "start", [P, K])
            end = sb(c, "end", [P, K])
            tmp = sb(c, "tmp", [P, K])
            hi_i = sb(c, "hi_i", [P, 1], I32)
            hi = sb(c, "hi", [P, 1])
            lastq = sb(c, "lastq", [P, 1])
            valid = sb(c, "valid", [P, 1])
            trash_i = sb(c, "trash_i", [P, 1], I32)
            s_x0, s_x, s_dst, s_src, s_zero, s_iota, s_mask = (sem(n) for n in (
                "x_cleared", "x_loaded", "dst_loaded", "src_loaded", "zeros_set", "iota_done", "mask_done"))
            s_cast, s_row, s_rowc, s_smp, s_smpd = (sem(n) for n in (
                "dst_cast", "row_spread", "row_copied", "samples_cut", "samples_stored"))
            s_b1, s_b2, s_st, s_std, s_en, s_la, s_lad, s_i3, s_i3d, s_fill = (sem(n) for n in (
                "block_found", "run_found", "start_found", "start_stored", "end_loaded", "last_found",
                "last_stored", "idx3_made", "idx3_stored", "firstrows_cleared"))
            s_g1, s_g2, s_lq = (pool_dma_sem(n) for n in ("samples_gathered", "runs_gathered", "lastq_gathered"))
            block = c.enter_context(nc.Block())

            @block.sync
            def _(sp):
                sp.dma_start(dst_i[:, :], dst_c).then_inc(s_dst, 16)
                sp.wait_ge(s_iota, 1)
                sp.dma_start(prev0_i[1:P, :], dst_c[0:P - 1, L - 1:L]).then_inc(s_dst, 16)
                sp.dma_start(src_i[:, :], src_c).then_inc(s_src, 16)
                sp.dma_start(ety_i[:, :], ety_c).then_inc(s_src, 16)
                sp.wait_ge(s_smp, 1)
                sp.dma_start(smp_d[:, :], smp[:, :]).then_inc(s_smpd, 16)
                sp.wait_ge(s_i3, 1)
                sp.dma_start(idx3_d[:, :], src_i[:, :]).then_inc(s_i3d, 16)
                sp.wait_ge(s_st, 1)
                sp.dma_start(start_d.rearrange("(p k) f -> p (k f)", k=K), start[:, :]).then_inc(s_std, 16)
                sp.wait_ge(s_std, 16)
                sp.dma_start(end[0:P - 1, K - 1:K], start_d.rearrange("(p k) f -> p (k f)", k=K)[1:P, 0:1])\
                    .then_inc(s_en, 16)
                sp.wait_ge(s_la, 1)
                sp.dma_start(nodes(last_d), last_i[:, :]).then_inc(s_lad, 16)
                sp.wait_ge(s_i3d, 16)

            @block.scalar
            def _(act):
                xv = x_sb[:, :, :].rearrange("p k f -> p (k f)")
                rows = lambda a, b: x[a * K:b * K, :].rearrange("(p k) f -> p (k f)", k=K)
                act.wait_ge(s_x0, 1)
                act.dma_start(xv[0:96, :], rows(0, 96)).then_inc(s_x, 16)
                act.dma_start(xv[96:126, :], rows(96, 126)).then_inc(s_x, 16)
                act.dma_start(xv[126:127, :], rows(126, 127)).then_inc(s_x, 16)
                rest = N - 127 * K
                act.dma_start(xv[127:128, 0:rest * D],
                              x[127 * K:N, :].rearrange("(p k) f -> p (k f)", k=rest)).then_inc(s_x, 16)
                act.wait_ge(s_zero, 1)
                fr = firstrows_d.rearrange("(p l) f -> p (l f)", p=P)
                for b in range(32):
                    act.dma_start(fr[:, b * 6250:(b + 1) * 6250], zeros[:, 0:6250]).then_inc(s_fill, 16)
                act.dma_start(firstad_d.rearrange("(p l) f -> p (l f)", p=P), zeros[:, 0:L]).then_inc(s_fill, 16)
                act.wait_ge(s_fill, 33 * 16)
                act.wait_ge(s_x, 64)

            @block.gpsimd
            def _(pool):
                step = Steps(pool, s_mask)
                pool.iota(nid_i[:, :], [[1, K]], base=0, channel_multiplier=K)
                pool.iota(hi_i[:, :], [[0, 1]], base=L, channel_multiplier=L)
                pool.iota(trash_i[:, :], [[0, 1]], base=NP, channel_multiplier=1)
                pool.memset(prev0_i[:, :], -1).then_inc(s_iota, 1)
                step(pool.memset(ident[:, :], 0.0))
                step(pool.memset(below[:, :], 1.0))
                step(pool.memset(above[:, :], 1.0))
                step(pool.memset(ones[:, :], 1.0))
                step(pool.affine_select(out=ident[:, :], in_=ident[:, :], compare_op=ALU.not_equal, fill=1.0,
                                        base=0, pattern=[[-1, P]], channel_multiplier=1))
                step(pool.affine_select(out=below[:, :], in_=below[:, :], compare_op=ALU.is_gt, fill=0.0,
                                        base=0, pattern=[[-1, P]], channel_multiplier=1))
                step(pool.affine_select(out=above[:, :], in_=above[:, :], compare_op=ALU.is_gt, fill=0.0,
                                        base=0, pattern=[[1, P]], channel_multiplier=-1))
                pool.wait_ge(s_zero, 1)
                for a in range(ACCS):
                    pool.dma_start(acc_d[a].rearrange("(p q) f -> p (q f)", p=P), zeros[:, :])\
                        .then_inc(acc_landed[a], 16)
                pool.wait_ge(s_smpd, 16)
                pool.wait_ge(s_b1, 1)
                for k in range(K):
                    pool.indirect_dma_start(
                        out=big[:, k * NSMP:(k + 1) * NSMP], out_offset=None, in_=smp_d,
                        in_offset=bass.IndirectOffsetOnAxis(ap=blk_i[:, k:k + 1], axis=0)).then_inc(s_g1, 16)
                pool.wait_ge(s_b2, 1)
                runs = dst.rearrange("(a b) -> a b", b=T)
                bigi = big[:, :].bitcast(I32)
                for k in range(K):
                    pool.indirect_dma_start(
                        out=bigi[:, k * T:(k + 1) * T], out_offset=None, in_=runs,
                        in_offset=bass.IndirectOffsetOnAxis(ap=blk_i[:, k:k + 1], axis=0)).then_inc(s_g2, 16)
                pool.wait_ge(s_lad, 16)
                pool.indirect_dma_start(
                    out=lastq_i[:, :], out_offset=None, in_=last_d,
                    in_offset=bass.IndirectOffsetOnAxis(ap=dst_i[:, 0:1], axis=0)).then_inc(s_lq, 16)
                for a in range(ACCS):
                    pool.wait_ge(acc_landed[a], 16)

            @block.tensor
            def _(pe):
                pe.wait_ge(s_cast, 1)
                pe.wait_ge(s_mask, 7)
                pe.matmul(bank[0][:, 0:P], lhsT=dstf[:, 0:1].to_broadcast([P, P]), rhs=ident[:, :],
                          start=True, stop=True)
                pe.matmul(bank[1][:, 0:P], lhsT=dstf[:, L - 1:L].to_broadcast([P, P]), rhs=ident[:, :],
                          start=True, stop=True).then_inc(s_row, 1)

            @block.vector
            def _(dve):
                step = Steps(dve, sem("order_setup"))
                dve.memset(x_sb[:, :, :], 0.0).then_inc(s_x0, 1)
                dve.memset(zeros[:, :], 0.0).then_inc(s_zero, 1)
                dve.wait_ge(s_dst, 32)
                step(dve.tensor_copy(dstf[:, :], dst_i[:, :]))
                step(dve.tensor_copy(smp[:, :], dstf[:, 0:L:T]))
                dve.tensor_copy(prev0[:, :], prev0_i[:, :]).then_inc(s_smp, 1)
                dve.tensor_copy(head_i[:, :], dst_i[:, 0:1]).then_inc(s_cast, 1)
                dve.wait_ge(s_smp, 1)
                dve.wait_ge(s_iota, 1)
                step(dve.tensor_tensor(cont[:, 1:L], dstf[:, 1:L], dstf[:, 0:L - 1], ALU.is_equal))
                step(dve.tensor_tensor(cont[:, 0:1], dstf[:, 0:1], prev0[:, :], ALU.is_equal))
                step(dve.tensor_copy(nid[:, :], nid_i[:, :]))
                step(dve.tensor_scalar(real[:, :], nid[:, :], float(N), None, ALU.is_lt))
                step(dve.tensor_copy(hi[:, :], hi_i[:, :]))
                step(dve.tensor_copy(trash[:, :], trash_i[:, :]))
                dve.wait_ge(s_row, 1)
                step(dve.tensor_copy(frow[:, :], bank[0][:, 0:P]))
                cmp1 = big[:, :].rearrange("p (k q) -> p k q", q=P)
                step(dve.tensor_tensor(cmp1, bc(frow[:, :], 1, [P, K, P]), bc(nid[:, :], 2, [P, K, P]), ALU.is_lt))
                step(dve.tensor_reduce(cnt[:, :], cmp1, AX, ALU.add))
                step(dve.tensor_scalar(blk[:, :], cnt[:, :], 1.0, 0.0, ALU.subtract, ALU.max))
                dve.tensor_copy(blk_i[:, :], blk[:, :]).then_inc(s_b1, 1)
                step(dve.scalar_tensor_tensor(carryT[:, :], bank[1][:, 0:P], dstf[:, 0:1], below[:, :],
                                              ALU.is_equal, ALU.mult))
                dve.wait_ge(s_src, 32)
                dve.scalar_tensor_tensor(src_i[:, :], src_i[:, :], float(R), ety_i[:, :], ALU.mult, ALU.add)\
                    .then_inc(s_i3, 1)
                dve.wait_ge(s_g1, 16 * K)
                smps = big[:, 0:K * NSMP].rearrange("p (k q) -> p k q", q=NSMP)
                step(dve.tensor_tensor(smps, smps, bc(nid[:, :], 2, [P, K, NSMP]), ALU.is_lt))
                step(dve.tensor_reduce(cnt[:, :], smps, AX, ALU.add))
                step(dve.tensor_scalar(cnt[:, :], cnt[:, :], 1.0, 0.0, ALU.subtract, ALU.max))
                step(dve.scalar_tensor_tensor(blk[:, :], blk[:, :], float(NSMP), cnt[:, :], ALU.mult, ALU.add))
                dve.tensor_copy(blk_i[:, :], blk[:, :]).then_inc(s_b2, 1)
                dve.wait_ge(s_g2, 16 * K)
                runs = big[:, 0:K * T].bitcast(I32).rearrange("p (k q) -> p k q", q=T)
                lt = big[:, K * T:2 * K * T].rearrange("p (k q) -> p k q", q=T)
                step(dve.tensor_copy(lt, runs))
                step(dve.tensor_tensor(lt, lt, bc(nid[:, :], 2, [P, K, T]), ALU.is_lt))
                step(dve.tensor_reduce(cnt[:, :], lt, AX, ALU.add))
                step(dve.scalar_tensor_tensor(start[:, :], blk[:, :], float(T), cnt[:, :], ALU.mult, ALU.add))
                step(dve.memset(end[:, K - 1:K], float(E)))
                dve.tensor_copy(end[:, 0:K - 1], start[:, 1:K]).then_inc(s_st, 1)
                dve.wait_ge(s_en, 16)
                dve.wait_ge(s_st, 1)
                step(dve.tensor_tensor(nonempty[:, :], end[:, :], start[:, :], ALU.is_gt))
                step(dve.tensor_scalar(end[:, :], end[:, :], 1.0, 0.0, ALU.subtract, ALU.max))
                dve.tensor_copy(last_i[:, :], end[:, :]).then_inc(s_la, 1)
                step(dve.tensor_scalar(tmp[:, :], nonempty[:, :], -SKIP, SKIP, ALU.mult, ALU.add))
                step(dve.tensor_tensor(tmp[:, :], tmp[:, :], start[:, :], ALU.add))
                step(dve.tensor_copy(first_i[:, :], tmp[:, :]))
                dve.wait_ge(s_lq, 16)
                step(dve.tensor_copy(lastq[:, :], lastq_i[:, :]))
                step(dve.tensor_tensor(valid[:, :], lastq[:, :], hi[:, :], ALU.is_lt))
                step(dve.tensor_scalar(valid[:, :], valid[:, :], -SKIP, SKIP, ALU.mult, ALU.add))
                step(dve.tensor_tensor(lastq[:, :], lastq[:, :], valid[:, :], ALU.add))
                step(dve.tensor_copy(fix_i[:, :], lastq[:, :]))

        def project(tag, h_in, w, bias, cols, tab, off):
            with phase() as c:
                s_cut, s_t, s_lo, s_hi, s_mm, s_o = (sem(f"{tag}_{n}") for n in (
                    "cut", "turned", "low_copied", "high_copied", "multiplied", "put"))
                xc = sb(c, f"{tag}_xc", [P, 2 * D])
                xT = sb(c, f"{tag}_xT", [D, 2 * P])
                xf = h_in[:, :, :].rearrange("p k f -> p (k f)")
                psT, psO = bank[0], bank[1][:, 0:2 * cols].rearrange("p (k f) -> p k f", k=2)
                block = c.enter_context(nc.Block())

                @block.gpsimd
                def _(pool):
                    with pool.Fori(0, K // 2) as i:
                        hold(pool, s_t, i + 1)
                        pool.tensor_copy(xc[:, :], xf[:, bass.ds(i * (2 * D), 2 * D)]).then_inc(s_cut, 1)

                @block.tensor
                def _(pe):
                    pe.sem_inc(s_t, 1)
                    with pe.Fori(0, K // 2) as i:
                        hold(pe, s_cut, i + 1)
                        pe.transpose(psT[:, 0:P], xc[:, :], ident[:, :]).then_inc(s_t, 1)
                        hold(pe, s_lo, i + 1)
                        hold(pe, s_hi, i + 1)
                        hold(pe, s_o, i + 1)
                        for h in range(2):
                            last = pe.matmul(psO[:, h, :], lhsT=xT[:, h * P:(h + 1) * P], rhs=w,
                                             start=True, stop=True)
                        last.then_inc(s_mm, 1)

                @block.scalar
                def _(act):
                    with act.Fori(0, K // 2) as i:
                        act.wait_ge(s_t, i + 2)
                        act.activation(xT[:, 0:P], psT[0:D, 0:P], ACT.Copy).then_inc(s_lo, 1)

                @block.vector
                def _(dve):
                    dve.sem_inc(s_o, 1)
                    with dve.Fori(0, K // 2) as i:
                        dve.wait_ge(s_t, i + 2)
                        dve.tensor_copy(xT[:, P:2 * P], psT[D:2 * D, 0:P]).then_inc(s_hi, 1)
                        dve.wait_ge(s_mm, i + 1)
                        dve.tensor_tensor(tab[:, bass.ds(i * 2, 2), off:off + cols], psO,
                                          bc(bias, 1, [P, 2, cols]), ALU.add).then_inc(s_o, 1)

        def layernorm(dve, act, step, sq, m, s_var, s_std, part):
            if part == "act":
                act.wait_ge(s_var, 1)
                act.activation(m[:, :], m[:, :], ACT.Sqrt).then_inc(s_std, 1)
                return
            step(dve.tensor_reduce(m[:, :], x_sb[:, :, :], AX, ALU.add))
            step(dve.tensor_scalar(m[:, :], m[:, :], 1.0 / D, None, ALU.mult))
            step(dve.tensor_tensor(x_sb[:, :, :], x_sb[:, :, :], bc(m[:, :], 2, [P, K, D]), ALU.subtract))
            step(dve.tensor_tensor(sq, x_sb[:, :, :], x_sb[:, :, :], ALU.mult))
            step(dve.tensor_reduce(m[:, :], sq, AX, ALU.add))
            dve.tensor_scalar(m[:, :], m[:, :], 1.0 / D, LN_EPS, ALU.mult, ALU.add).then_inc(s_var, 1)
            dve.wait_ge(s_std, 1)
            step(dve.reciprocal(m[:, :], m[:, :]))
            step(dve.tensor_tensor(x_sb[:, :, :], x_sb[:, :, :], bc(m[:, :], 2, [P, K, D]), ALU.mult))

        def row(c, name, vec, cols=D):
            t = sb(c, name, [P, cols])
            return t, (t[:, :], bc(vec, 0, [P, cols]))

        w0 = ExitStack()
        w_pair = sb(w0, "w_pair", [D, 2 * D + 2 * D])
        w_ig = sb(w0, "w_ig", [D, 2 * D])
        bias_ig = sb(w0, "bias_ig", [1, GRP, 2 * D])
        bias_pair = sb(w0, "bias_pair", [P, 2 * D])
        with phase() as c:
            wg = sb(c, "wg", [D, D])
            w2T = sb(c, "w2T", [D, D])
            b2c = sb(c, "b2c", [D, 1])
            b2r = sb(c, "b2r", [1, 2 * D])
            s_w, s_bz, s_t, s_tc, s_g = (sem(f"l0w_{n}") for n in ("loaded", "cleared", "turned", "copied", "product"))
            block = c.enter_context(nc.Block())

            @block.sync
            def _(sp):
                sp.dma_start(w_pair[:, 0:D], W["L0_gnn_W1"][0:D, :]).then_inc(s_w, 16)
                sp.dma_start(w_pair[:, D:2 * D], W["L0_gnn_W1"][D:2 * D, :]).then_inc(s_w, 16)
                sp.dma_start(w_ig[:, 0:D], W["L0_gnn_W2"]).then_inc(s_w, 16)
                sp.dma_start(wg[:, :], W["L0_gnn_Wg"]).then_inc(s_w, 16)
                sp.dma_start(b2c[:, :], W["L0_gnn_b2"].unsqueeze(1)).then_inc(s_w, 16)
                sp.dma_start(b2r[:, 0:D], W["L0_gnn_b2"].unsqueeze(0)).then_inc(s_w, 16)
                sp.dma_start(b2r[:, D:2 * D], W["L0_gnn_bg"].unsqueeze(0)).then_inc(s_w, 16)
                sp.dma_start(bias_pair[:, D:2 * D], bc(W["L0_gnn_b1"], 0, [P, D])).then_inc(s_w, 16)

            @block.tensor
            def _(pe):
                pe.wait_ge(s_w, 128)
                pe.transpose(bank[0][0:D, 0:D], w_ig[:, 0:D], ident[0:D, 0:D]).then_inc(s_t, 1)
                pe.matmul(bank[1][0:1, 0:D], lhsT=b2c[:, :], rhs=wg[:, :], start=True, stop=True).then_inc(s_t, 1)
                pe.wait_ge(s_tc, 1)
                pe.matmul(bank[2][0:D, 0:D], lhsT=w2T[:, :], rhs=wg[:, :], start=True, stop=True).then_inc(s_g, 1)

            @block.vector
            def _(dve):
                step = Steps(dve, sem("order_l0w"))
                step(dve.memset(bias_pair[:, 0:D], 0.0))
                dve.wait_ge(s_w, 128)
                dve.wait_ge(s_t, 2)
                dve.tensor_copy(w2T[:, :], bank[0][0:D, 0:D]).then_inc(s_tc, 1)
                step(dve.tensor_tensor(b2r[:, D:2 * D], b2r[:, D:2 * D], bank[1][0:1, 0:D], ALU.add))
                for g in range(GRP):
                    dve.tensor_copy(bias_ig[:, g, :], b2r[:, :])
                dve.wait_ge(s_g, 1)
                step(dve.tensor_copy(w_ig[:, D:2 * D], bank[2][0:D, 0:D]))

        head0 = sb(w0, "head0", [P, D])
        with phase() as c:
            tab = sb(c, "tab0", [P, K, 2 * D])
            project("pair", x_sb, w_pair[:, 0:2 * D], bias_pair[:, :], 2 * D, tab, 0)
            s_tab, s_sc, s_hd = sem("pair_stored"), pool_dma_sem("pair_scattered"), pool_dma_sem("pair_heads")
            block = c.enter_context(nc.Block())

            @block.sync
            def _(sp):
                tv = lambda ap: ap.rearrange("(p k) f -> p k f", k=K)
                sp.dma_start(tv(tabA_d), tab[:, :, 0:D]).then_inc(s_tab, 16)
                sp.dma_start(tv(tabB_d), tab[:, :, D:2 * D]).then_inc(s_tab, 16)
                sp.wait_ge(s_tab, 32)

            @block.gpsimd
            def _(pool):
                for k in range(K):
                    pool.indirect_dma_start(
                        out=firstrows_d, out_offset=bass.IndirectOffsetOnAxis(ap=first_i[:, k:k + 1], axis=0),
                        in_=tab[:, k, D:2 * D], in_offset=None,
                        bounds_check=E - 1, oob_is_err=False).then_inc(s_sc, 16)
                pool.wait_ge(s_tab, 32)
                pool.indirect_dma_start(
                    out=head0[:, :], out_offset=None, in_=tabB_d,
                    in_offset=bass.IndirectOffsetOnAxis(ap=head_i[:, 0:1], axis=0)).then_inc(s_hd, 16)
                pool.wait_ge(s_sc, 16 * K)
                pool.wait_ge(s_hd, 16)

        with phase() as c:
            idx = [sb(c, f"idx{r}", [P, T], I32) for r in range(RING)]
            G = [sb(c, f"G{r}", [P, T, D]) for r in range(RING)]
            Br = [sb(c, f"Br{r}", [P, T, D]) for r in range(RING)]
            sums = [sb(c, f"sums{r}", [P, T, D + 1]) for r in range(RING)]
            idxs = [sb(c, f"idxs{r}", [P, T], I32) for r in range(RING)]
            srcf = sb(c, "srcf", [P, T])
            contc = sb(c, "contc", [P, T])
            keep = sb(c, "keep", [P, D, T])
            BT = sb(c, "BT", [P, D, T])
            F = sb(c, "F", [P, D, T])
            H = sb(c, "H", [P, T, D])
            HT = sb(c, "HT", [D, GRP * P])
            gate = sb(c, "gate", [P, GRP, D])
            msg = [sb(c, f"msg{b}", [P, GRP, D + 1]) for b in range(2)]
            same = [sb(c, f"same{b}", [P, GRP, P]) for b in range(2)]
            earlier = sb(c, "earlier", [P, GRP, P])
            dup = sb(c, "dup", [P, T])
            to = sb(c, "to", [P, T])
            s_idx = [sem(f"e0_idx{r}") for r in range(RING)]
            s_g = [pool_dma_sem(f"e0_gathered{r}") for r in range(RING)]
            s_br = [sem(f"e0_first_rows{r}") for r in range(RING)]
            (s_brf, s_bt, s_F, s_H, s_T, s_HT, s_I, s_sg, s_B, s_eq, s_C, s_Co, s_to, s_ini) = (
                sem(f"e0_{n}") for n in (
                    "first_rows_free", "first_rows_turned", "filled", "added", "turned", "relu_done",
                    "interaction", "gate_done", "sources_spread", "message_done", "combined", "combined_copied",
                    "targets_done", "started"))
            block = c.enter_context(nc.Block())
            first_v = firstrows_d.rearrange("(p l) f -> p (l f)", p=P)

            @block.sync
            def _(sp):
                def body(j, r, n):
                    sp.wait_ge(s_to, j + 1)
                    sp.dma_start(idx[r][:, :], src_c[:, bass.ds(j * T, T)]).then_inc(s_idx[r], 16)
                    sp.wait_ge(s_brf, j + 1)
                    sp.dma_start(Br[r][:, :, :].rearrange("p t f -> p (t f)"),
                                 first_v[:, bass.ds(j * (T * D), T * D)]).then_inc(s_br[r], 16)
                chunk_loop(sp, body)

            @block.gpsimd
            def _(pool):
                def gather(j, r, n, t):
                    pool.indirect_dma_start(
                        out=G[r][:, t, :], out_offset=None, in_=tabA_d,
                        in_offset=bass.IndirectOffsetOnAxis(ap=idx[r][:, t:t + 1], axis=0)).then_inc(s_g[r], 16)

                def scatter(j, r, t):
                    hold(pool, acc_landed[t % ACCS], j * (16 * T // ACCS) + 16 * (1 + t // ACCS))
                    pool.indirect_dma_start(
                        out=acc_d[t % ACCS], out_offset=bass.IndirectOffsetOnAxis(ap=idxs[r][:, t:t + 1], axis=0),
                        in_=sums[r][:, t, :], in_offset=None, compute_op=ALU.add).then_inc(acc_landed[t % ACCS], 16)

                def ready(j):
                    hold(pool, s_to, j + (1 + RING))
                    hold(pool, s_Co, j * NG + (NG + 2))

                def body(j, r, n):
                    pool.wait_ge(s_idx[r], n * 16 + 16)
                    hold(pool, s_H, j + 1)
                    if since(j, LAG):
                        ready(j - LAG)
                    for t in range(T):
                        gather(j, r, n, t)
                        if since(j, LAG):
                            scatter(j - LAG, (r - LAG) % RING, t)
                chunk_loop(pool, body)
                for j in range(CH - LAG, CH):
                    ready(j)
                    for t in range(T):
                        scatter(j, j % RING, t)
                for a in range(ACCS):
                    pool.wait_ge(acc_landed[a], 16 * (1 + CH * T // ACCS))

            @block.scalar
            def _(act):
                act.sem_inc(s_brf, RING)
                act.sem_inc(s_Co, 2)
                act.wait_ge(s_ini, 1)

                def relu(j, g):
                    n = GROUPS[g][1] * P
                    act.wait_ge(s_T, j * NG + (g + 1))
                    act.activation(HT[:, 0:n], bank[0][0:D, 0:n], ACT.Relu).then_inc(s_HT, 1)

                def body(j, r, n):
                    act.wait_ge(s_br[r], n * 16 + 16)
                    hold(act, s_F, j + 1)
                    act.activation(BT[:, :, :].rearrange("p f t -> p t f"), Br[r][:, :, :], ACT.Copy).then_inc(s_brf, 1)
                    act.activation(keep[:, :, 1:T],
                                   bc(cont[:, bass.ds(j * T + 1, T - 1)], 1, [P, D, T - 1]), ACT.Copy).then_inc(s_bt, 1)
                    relu(j, 0)
                    for g, (t0, m) in enumerate(GROUPS):
                        act.wait_ge(s_I, j * NG + (g + 1))
                        psI = bank[1][:, 0:m * 2 * D].rearrange("p (t f) -> p t f", t=m)
                        act.activation(gate[:, 0:m, :], psI[:, :, D:2 * D], ACT.Sigmoid).then_inc(s_sg, 1)
                        if g + 1 < NG:
                            relu(j, g + 1)
                        act.wait_ge(s_C, j * NG + (g + 1))
                        if g == 0 and since(j, RING):
                            for a in range(ACCS):
                                act.wait_ge(acc_landed[a], (j - (RING - 1)) * (16 * T // ACCS) + 16)
                        psC = bank[4 + g % 2][:, 0:m * (D + 1)].rearrange("p (t f) -> p t f", t=m)
                        act.activation(sums[r][:, t0:t0 + m, :], psC, ACT.Copy).then_inc(s_Co, 1)
                chunk_loop(act, body)

            @block.tensor
            def _(pe):
                def turn(j, g):
                    t0, m = GROUPS[g]
                    for t in range(m):
                        last = pe.transpose(bank[0][0:D, t * P:(t + 1) * P], H[:, t0 + t, :], ident[:, :])
                    last.then_inc(s_T, 1)
                    for t in range(m):
                        last = pe.matmul(bank[2 + g % 2][:, t * P:(t + 1) * P],
                                         lhsT=srcf[:, t0 + t:t0 + t + 1].to_broadcast([P, P]), rhs=ident[:, :],
                                         start=True, stop=True)
                    last.then_inc(s_B, 1)

                def body(j, r, n):
                    hold(pe, s_H, j + (1 + RING))
                    turn(j, 0)
                    for g, (t0, m) in enumerate(GROUPS):
                        hold(pe, s_HT, j * NG + (g + 1))
                        pe.matmul(bank[1][:, 0:m * 2 * D], lhsT=ones[0:1, :],
                                  rhs=bias_ig[:, 0:m, :].rearrange("p t f -> p (t f)"), start=True, stop=False)
                        for t in range(m):
                            last = pe.matmul(bank[1][:, t * 2 * D:(t + 1) * 2 * D], lhsT=HT[:, t * P:(t + 1) * P],
                                             rhs=w_ig[:, :], start=False, stop=(t == m - 1))
                        last.then_inc(s_I, 1)
                        if g + 1 < NG:
                            turn(j, g + 1)
                        hold(pe, s_eq, j * NG + (g + 1))
                        hold(pe, s_Co, j * NG + (g + 1))
                        for t in range(m):
                            last = pe.matmul(bank[4 + g % 2][:, t * (D + 1):(t + 1) * (D + 1)],
                                             lhsT=same[g % 2][:, t, :], rhs=msg[g % 2][:, t, :],
                                             start=True, stop=True)
                        last.then_inc(s_C, 1)
                chunk_loop(pe, body)

            @block.vector
            def _(dve):
                step = Steps(dve, sem("order_e0"))
                dve.sem_inc(s_H, RING)
                dve.sem_inc(s_to, RING)
                step(dve.memset(F[:, :, :], 0.0))
                step(dve.tensor_copy(F[:, :, T - 1], head0[:, :]))
                for b in range(2):
                    step(dve.memset(msg[b][:, :, :], 1.0))
                dve.memset(keep[:, :, :], 0.0).then_inc(s_ini, 1)
                dve.sem_inc(s_F, 1)

                def body(j, r, n):
                    step.chunk(j, 7 + 2 * NG)
                    dve.wait_ge(s_idx[r], n * 16 + 16)
                    step(dve.tensor_copy(srcf[:, :], idx[r][:, :]))
                    step(dve.tensor_scalar(contc[:, :], cont[:, bass.ds(j * T, T)], 1.0, None, ALU.mult))
                    dve.wait_ge(s_bt, j + 1)
                    step(dve.scalar_tensor_tensor(BT[:, :, 0], F[:, :, T - 1], contc[:, 0:1],
                                                  BT[:, :, 0], ALU.mult, ALU.add))
                    flat = lambda ap: ap[:, :, :].rearrange("p f t -> p (f t)")
                    dve.tensor_tensor_scan(flat(F), flat(keep), flat(BT), 0.0, ALU.mult, ALU.add).then_inc(s_F, 1)
                    dve.wait_ge(s_g[r], n * (16 * T) + 16 * T)
                    dve.wait_ge(s_F, j + 2)
                    dve.tensor_tensor(H[:, :, :], G[r][:, :, :], F[:, :, :].rearrange("p f t -> p t f"),
                                      ALU.add).then_inc(s_H, 1)
                    for g, (t0, m) in enumerate(GROUPS):
                        b = g % 2
                        dve.wait_ge(s_B, j * NG + (g + 1))
                        step(dve.tensor_tensor(same[b][:, 0:m, :],
                                               bank[2 + b][:, 0:m * P].rearrange("p (t q) -> p t q", t=m),
                                               bc(srcf[:, t0:t0 + m], 2, [P, m, P]), ALU.is_equal))
                        step(dve.tensor_tensor(earlier[:, 0:m, :], same[b][:, 0:m, :],
                                               bc(below[:, :], 1, [P, m, P]), ALU.mult))
                        dve.tensor_reduce(dup[:, t0:t0 + m], earlier[:, 0:m, :], AX, ALU.add)
                        dve.wait_ge(s_sg, j * NG + (g + 1))
                        psI = bank[1][:, 0:m * 2 * D].rearrange("p (t f) -> p t f", t=m)
                        dve.tensor_tensor(msg[b][:, 0:m, 0:D], psI[:, :, 0:D], gate[:, 0:m, :],
                                          ALU.mult).then_inc(s_eq, 1)
                    dve.wait_ge(s_eq, j * NG + NG)
                    step(dve.tensor_scalar(dup[:, :], dup[:, :], 0.5, None, ALU.is_gt))
                    step(dve.tensor_scalar(to[:, :], srcf[:, :], -1.0, trash[:, 0:1], ALU.mult, ALU.add))
                    step(dve.tensor_tensor(to[:, :], to[:, :], dup[:, :], ALU.mult))
                    step(dve.tensor_tensor(to[:, :], to[:, :], srcf[:, :], ALU.add))
                    if since(j, RING):
                        for a in range(ACCS):
                            dve.wait_ge(acc_landed[a], (j - (RING - 1)) * (16 * T // ACCS) + 16)
                    dve.tensor_copy(idxs[r][:, :], to[:, :]).then_inc(s_to, 1)
                    step.end_chunk()
                chunk_loop(dve, body)

        with phase() as c:
            A = [sb(c, f"A{a}", [P, K, D + 1]) for a in range(ACCS)]
            m = sb(c, "m0", [P, K])
            s_a, s_var, s_std = sem("n0_loaded"), sem("n0_var"), sem("n0_std")
            block = c.enter_context(nc.Block())

            @block.sync
            def _(sp):
                for a in range(ACCS):
                    sp.dma_start(A[a][:, :, :].rearrange("p k f -> p (k f)"),
                                 nodes(acc_d[a][0:NP, :])).then_inc(s_a, 16)

            @block.scalar
            def _(act):
                layernorm(None, act, None, None, m, s_var, s_std, "act")

            @block.vector
            def _(dve):
                step = Steps(dve, sem("order_n0"))
                dve.wait_ge(s_a, 16 * ACCS)
                for a in range(1, ACCS):
                    step(dve.tensor_tensor(A[0][:, :, :], A[0][:, :, :], A[a][:, :, :], ALU.add))
                step(dve.tensor_scalar(m[:, :], A[0][:, :, D], 1.0, None, ALU.max))
                step(dve.reciprocal(m[:, :], m[:, :]))
                step(dve.tensor_tensor(A[0][:, :, 0:D], A[0][:, :, 0:D], bc(m[:, :], 2, [P, K, D]), ALU.mult))
                step(dve.tensor_tensor(x_sb[:, :, :], x_sb[:, :, :], A[0][:, :, 0:D], ALU.add))
                layernorm(dve, None, step, A[1][:, :, 0:D], m, s_var, s_std, "dve")
        w0.close()

        def store_out():
            with phase() as c:
                s_out = sem("out_stored")
                block = c.enter_context(nc.Block())

                @block.sync
                def _(sp):
                    xv = x_sb[:, :, :].rearrange("p k f -> p (k f)")
                    rows = lambda a, b: out[a * K:b * K, :].rearrange("(p k) f -> p (k f)", k=K)
                    for a, b in ((0, 96), (96, 126), (126, 127)):
                        sp.dma_start(rows(a, b), xv[a:b, :]).then_inc(s_out, 16)
                    rest = N - 127 * K
                    sp.dma_start(out[127 * K:N, :].rearrange("(p k) f -> p (k f)", k=rest),
                                 xv[127:128, 0:rest * D]).then_inc(s_out, 16)
                    sp.wait_ge(s_out, 64)


        def segments(tag, kind, table, idx_src, head, wrow, fin):
            width = {"attn": ROW + D, "gat": ROW, "rel": D}[kind]
            chans = D if kind == "rel" else D + 1
            with phase() as c:
                idx = [sb(c, f"{tag}_idx{r}", [P, T], I32) for r in range(RING)]
                G = [sb(c, f"{tag}_G{r}", [P, T, width]) for r in range(RING)]
                rows = [sb(c, f"{tag}_rows{r}", [P, T, ROW]) for r in range(RING)]
                contc = sb(c, f"{tag}_contc", [P, T])
                reset = sb(c, f"{tag}_reset", [P, T])
                logit = sb(c, f"{tag}_logit", [P, T])
                top = sb(c, f"{tag}_top", [P, T + 1])
                arg = sb(c, f"{tag}_arg", [P, 2, T])
                wd = sb(c, f"{tag}_wd", [P, 2, T])
                decay = sb(c, f"{tag}_decay", [P, chans, T])
                V = sb(c, f"{tag}_V", [P, chans, T])
                O = sb(c, f"{tag}_O", [P, chans, T])
                if kind == "attn":
                    Br = [sb(c, f"{tag}_Br{r}", [P, T, D]) for r in range(RING)]
                    keep = sb(c, f"{tag}_keep", [P, D, T])
                    BT = sb(c, f"{tag}_BT", [P, D, T])
                    F = sb(c, f"{tag}_F", [P, D, T])
                    H = sb(c, f"{tag}_H", [P, T, D])
                if kind == "gat":
                    adst = sb(c, f"{tag}_adst", [P, L])
                if kind == "rel":
                    norm = [sb(c, f"{tag}_norm{r}", [P, T]) for r in range(RING)]
                s_idx = [sem(f"{tag}_idx_loaded{r}") for r in range(RING)]
                s_g = [pool_dma_sem(f"{tag}_gathered{r}") for r in range(RING)]
                s_st = [sem(f"{tag}_rows_stored{r}") for r in range(RING)]
                s_br = [sem(f"{tag}_first_rows{r}") for r in range(RING)]
                (s_used, s_turn, s_F, s_H, s_tanh, s_arg, s_wd, s_dc, s_O, s_rows, s_ini, s_ad) = (
                    sem(f"{tag}_{n}") for n in (
                        "rows_used", "first_rows_turned", "filled", "added", "tanh_done", "args_done",
                        "weights_done", "decay_spread", "summed", "rows_made", "started", "adst_loaded"))
                block = c.enter_context(nc.Block())
                first_v = firstrows_d.rearrange("(p l) f -> p (l f)", p=P)
                state_v = state_d.rearrange("(p l) f -> p (l f)", p=P)
                norm_v = ew.rearrange("(p l) f -> p (l f)", p=P)
                flat = lambda ap: ap[:, :, :].rearrange("p f t -> p (f t)")

                @block.sync
                def _(sp):
                    if kind == "gat":
                        sp.dma_start(adst[:, :], firstad_d.rearrange("(p l) f -> p (l f)", p=P)).then_inc(s_ad, 16)

                    def body(j, r, n):
                        if since(j, RING):
                            sp.wait_ge(s_used, j - (RING - 1))
                        sp.dma_start(idx[r][:, :], idx_src[:, bass.ds(j * T, T)]).then_inc(s_idx[r], 16)
                        if kind == "rel":
                            sp.dma_start(norm[r][:, :], norm_v[:, bass.ds(j * T, T)]).then_inc(s_br[r], 16)
                        if kind == "attn":
                            if since(j, RING):
                                sp.wait_ge(s_turn, j - (RING - 1))
                            sp.dma_start(Br[r][:, :, :].rearrange("p t f -> p (t f)"),
                                         first_v[:, bass.ds(j * (T * D), T * D)]).then_inc(s_br[r], 16)
                    chunk_loop(sp, body)

                @block.gpsimd
                def _(pool):
                    def body(j, r, n):
                        hold(pool, s_idx[r], n * 16 + 16)
                        if since(j, RING):
                            hold(pool, s_used, j - (RING - 1))
                        for t in range(T):
                            pool.indirect_dma_start(
                                out=G[r][:, t, :], out_offset=None, in_=table,
                                in_offset=bass.IndirectOffsetOnAxis(ap=idx[r][:, t:t + 1], axis=0))\
                                .then_inc(s_g[r], 16)
                    chunk_loop(pool, body)

                @block.scalar
                def _(act):
                    act.wait_ge(s_ini, 1)

                    def body(j, r, n):
                        if kind == "attn":
                            act.wait_ge(s_br[r], n * 16 + 16)
                            if since(j, 1):
                                hold(act, s_F, j)
                            act.activation(BT[:, :, :].rearrange("p f t -> p t f"), Br[r][:, :, :], ACT.Copy)
                            act.activation(keep[:, :, 1:T],
                                           bc(cont[:, bass.ds(j * T + 1, T - 1)], 1, [P, D, T - 1]),
                                           ACT.Copy).then_inc(s_turn, 1)
                            act.wait_ge(s_H, j + 1)
                            act.activation(H[:, :, :], H[:, :, :], ACT.Tanh).then_inc(s_tanh, 1)
                        act.wait_ge(s_arg, j + 1)
                        if kind != "rel":
                            act.activation(wd[:, :, :], arg[:, :, :], ACT.Exp).then_inc(s_wd, 1)
                            act.wait_ge(s_wd, j + 1)
                        act.activation(decay[:, :, 1:T],
                                       bc(wd[:, 0, 1:T], 1, [P, chans, T - 1]), ACT.Copy).then_inc(s_dc, 1)
                        if since(j, RING):
                            act.wait_ge(s_st[r], n * 16)
                        act.wait_ge(s_O, j + 1)
                        act.activation(rows[r][:, :, 0:chans].rearrange("p t f -> p f t"), O[:, :, :], ACT.Copy)\
                            .then_inc(s_rows, 1)
                        if kind != "rel":
                            act.activation(rows[r][:, :, D + 1], top[:, 1:T + 1], ACT.Copy).then_inc(s_rows, 1)
                        act.wait_ge(s_rows, (j + 1) * (1 if kind == "rel" else 2))
                        act.dma_start(state_v[:, bass.ds(j * (T * ROW), T * ROW)],
                                      rows[r][:, :, :].rearrange("p t f -> p (t f)")).then_inc(s_st[r], 16)
                    chunk_loop(act, body)
                    for r in range(RING):
                        act.wait_ge(s_st[r], 16 * len(range(r, CH, RING)))

                @block.vector
                def _(dve):
                    step = Steps(dve, sem(f"order_{tag}"))
                    step(dve.memset(O[:, :, :], 0.0))
                    step(dve.memset(top[:, :], -BIG))
                    step(dve.memset(decay[:, :, :], 0.0))
                    if kind == "rel":
                        for r in range(RING):
                            step(dve.memset(rows[r][:, :, :], 0.0))
                    if kind == "attn":
                        step(dve.memset(F[:, :, :], 0.0))
                        step(dve.memset(keep[:, :, :], 0.0))
                        step(dve.tensor_copy(F[:, :, T - 1], head[:, :]))
                    if kind == "gat":
                        dve.wait_ge(s_ad, 16)
                        step(dve.tensor_tensor_scan(adst[:, :], cont[:, :], adst[:, :], head[:, 0:1],
                                                    ALU.mult, ALU.add))
                    dve.sem_inc(s_ini, 1)

                    def body(j, r, n):
                        step.chunk(j, {"attn": 11, "gat": 10, "rel": 3}[kind])
                        step(dve.tensor_scalar(contc[:, :], cont[:, bass.ds(j * T, T)], 1.0, None, ALU.mult))
                        if kind == "attn":
                            dve.wait_ge(s_turn, j + 1)
                            step(dve.scalar_tensor_tensor(BT[:, :, 0], F[:, :, T - 1], contc[:, 0:1],
                                                          BT[:, :, 0], ALU.mult, ALU.add))
                            dve.tensor_tensor_scan(flat(F), flat(keep), flat(BT), 0.0, ALU.mult, ALU.add)\
                                .then_inc(s_F, 1)
                            dve.wait_ge(s_F, j + 1)
                        dve.wait_ge(s_g[r], n * (16 * T) + 16 * T)
                        if kind == "attn":
                            dve.tensor_tensor(H[:, :, :], G[r][:, :, ROW:ROW + D],
                                              F[:, :, :].rearrange("p f t -> p t f"), ALU.add).then_inc(s_H, 1)
                            dve.wait_ge(s_tanh, j + 1)
                            step(dve.tensor_tensor(H[:, :, :], H[:, :, :], bc(wrow[:, :], 1, [P, T, D]), ALU.mult))
                            step(dve.tensor_reduce(logit[:, :], H[:, :, :], AX, ALU.add))
                        if kind == "gat":
                            step(dve.tensor_tensor(logit[:, :], adst[:, bass.ds(j * T, T)], G[r][:, :, D + 1],
                                                   ALU.add))
                            step(dve.scalar_tensor_tensor(logit[:, :], logit[:, :], NEG_SLOPE, logit[:, :],
                                                          ALU.mult, ALU.max))
                        if kind == "rel":
                            dve.tensor_copy(wd[:, 0, :], contc[:, :]).then_inc(s_arg, 1)
                            dve.wait_ge(s_br[r], n * 16 + 16)
                            weight = norm[r][:, :]
                        else:
                            if since(j, 1):
                                dve.wait_ge(s_rows, j * 2)
                            step(dve.tensor_scalar(reset[:, :], contc[:, :], 1.0, BIG, ALU.subtract, ALU.mult))
                            step(dve.tensor_copy(top[:, 0:1], top[:, T:T + 1]))
                            step(dve.tensor_tensor_scan(top[:, 1:T + 1], reset[:, :], logit[:, :], top[:, 0:1],
                                                        ALU.add, ALU.max))
                            step(dve.tensor_tensor(arg[:, 0, :], top[:, 0:T], reset[:, :], ALU.add))
                            step(dve.tensor_tensor(arg[:, 0, :], arg[:, 0, :], top[:, 1:T + 1], ALU.subtract))
                            dve.tensor_tensor(arg[:, 1, :], logit[:, :], top[:, 1:T + 1], ALU.subtract)\
                                .then_inc(s_arg, 1)
                            dve.wait_ge(s_wd, j + 1)
                            weight = wd[:, 1, :]
                        step(dve.tensor_tensor(V[:, :, :].rearrange("p f t -> p t f"), G[r][:, :, 0:chans],
                                               bc(weight, 2, [P, T, chans]), ALU.mult))
                        if kind == "rel":
                            dve.wait_ge(s_dc, j + 1)
                        step(dve.scalar_tensor_tensor(V[:, :, 0], O[:, :, T - 1], wd[:, 0, 0:1], V[:, :, 0],
                                                      ALU.mult, ALU.add))
                        dve.sem_inc(s_used, 1)
                        dve.wait_ge(s_dc, j + 1)
                        if kind == "rel" and since(j, 1):
                            dve.wait_ge(s_rows, j)
                        dve.tensor_tensor_scan(flat(O), flat(decay), flat(V), 0.0, ALU.mult, ALU.add)\
                            .then_inc(s_O, 1)
                        dve.wait_ge(s_O, j + 1)
                        step.end_chunk()
                    chunk_loop(dve, body)
                    step.end_loop(CH)
                    step(dve.memset(fin[:, :], 0.0))
                    step(dve.tensor_copy(fin[:, 0:chans], O[:, :, T - 1]))
                    if kind != "rel":
                        step(dve.tensor_copy(fin[:, D + 1:ROW], top[:, T:T + 1]))

        def finish_segments(tag, fin, S):
            with phase() as c:
                t1 = sb(c, f"{tag}_t1", [P, P])
                ex = sb(c, f"{tag}_ex", [P, P])
                exT = sb(c, f"{tag}_exT", [P, P])
                tops = sb(c, f"{tag}_tops", [P, 2])
                ab = sb(c, f"{tag}_ab", [P, 2])
                U = sb(c, f"{tag}_U", [P, ROW])
                s_row, s_d, s_ex, s_m, s_t, s_c, s_in, s_ab, s_eab, s_new = (
                    sem(f"{tag}_{n}") for n in (
                        "tops_spread", "tops_off", "exps", "masked", "turned", "turn_copied", "handed",
                        "offsets", "factors", "merged"))
                s_u, s_fix, s_all = (pool_dma_sem(f"{tag}_{n}") for n in ("last_rows", "fixed", "collected"))
                block = c.enter_context(nc.Block())

                @block.tensor
                def _(pe):
                    pe.matmul(bank[0][:, 0:P], lhsT=fin[:, D + 1:ROW].to_broadcast([P, P]), rhs=ident[:, :],
                              start=True, stop=True).then_inc(s_row, 1)
                    pe.wait_ge(s_m, 1)
                    pe.transpose(bank[1][:, 0:P], ex[:, :], ident[:, :]).then_inc(s_t, 1)
                    pe.wait_ge(s_c, 1)
                    pe.matmul(bank[2][:, 0:D + 1], lhsT=exT[:, :], rhs=fin[:, 0:D + 1],
                              start=True, stop=True).then_inc(s_in, 1)

                @block.scalar
                def _(act):
                    act.wait_ge(s_d, 1)
                    act.activation(ex[:, :], t1[:, :], ACT.Exp).then_inc(s_ex, 1)
                    act.wait_ge(s_ab, 1)
                    act.activation(ab[:, :], ab[:, :], ACT.Exp).then_inc(s_eab, 1)

                @block.gpsimd
                def _(pool):
                    pool.indirect_dma_start(out=U[:, :], out_offset=None, in_=state_d,
                                            in_offset=bass.IndirectOffsetOnAxis(ap=lastq_i[:, 0:1], axis=0))\
                        .then_inc(s_u, 16)
                    pool.wait_ge(s_new, 1)
                    pool.indirect_dma_start(out=state_d,
                                            out_offset=bass.IndirectOffsetOnAxis(ap=fix_i[:, 0:1], axis=0),
                                            in_=U[:, :], in_offset=None,
                                            bounds_check=E - 1, oob_is_err=False).then_inc(s_fix, 16)
                    pool.wait_ge(s_fix, 16)
                    for k in range(K):
                        pool.indirect_dma_start(out=S[:, k, :], out_offset=None, in_=state_d,
                                                in_offset=bass.IndirectOffsetOnAxis(ap=last_i[:, k:k + 1], axis=0))\
                            .then_inc(s_all, 16)
                    pool.wait_ge(s_all, 16 * K)

                @block.vector
                def _(dve):
                    step = Steps(dve, sem(f"order_{tag}"))
                    step(dve.tensor_scalar(t1[:, :], carryT[:, :], 1.0, BIG, ALU.subtract, ALU.mult))
                    dve.wait_ge(s_row, 1)
                    step(dve.tensor_tensor(t1[:, :], t1[:, :], bank[0][:, 0:P], ALU.add))
                    step(dve.tensor_reduce(tops[:, 0:1], t1[:, :], AX, ALU.max))
                    dve.tensor_scalar(t1[:, :], t1[:, :], tops[:, 0:1], None, ALU.subtract).then_inc(s_d, 1)
                    dve.wait_ge(s_ex, 1)
                    dve.tensor_tensor(ex[:, :], ex[:, :], carryT[:, :], ALU.mult).then_inc(s_m, 1)
                    dve.wait_ge(s_t, 1)
                    dve.tensor_copy(exT[:, :], bank[1][:, 0:P]).then_inc(s_c, 1)
                    dve.wait_ge(s_u, 16)
                    step(dve.tensor_tensor(tops[:, 1:2], tops[:, 0:1], U[:, D + 1:ROW], ALU.max))
                    step(dve.tensor_tensor(ab[:, 0:1], tops[:, 0:1], tops[:, 1:2], ALU.subtract))
                    dve.tensor_tensor(ab[:, 1:2], U[:, D + 1:ROW], tops[:, 1:2], ALU.subtract).then_inc(s_ab, 1)
                    dve.wait_ge(s_eab, 1)
                    step(dve.tensor_scalar(U[:, 0:D + 1], U[:, 0:D + 1], ab[:, 1:2], None, ALU.mult))
                    dve.wait_ge(s_in, 1)
                    step(dve.scalar_tensor_tensor(U[:, 0:D + 1], bank[2][:, 0:D + 1], ab[:, 0:1], U[:, 0:D + 1],
                                                  ALU.mult, ALU.add))
                    dve.tensor_copy(U[:, D + 1:ROW], tops[:, 1:2]).then_inc(s_new, 1)

        with phase() as w:
            w_attn = sb(w, "w_attn", [D, 2 * D])
            w_raw = sb(w, "w_raw", [D, 2 * D])
            bias1 = sb(w, "bias1", [P, 2 * D])
            wout = sb(w, "wout", [P, D])
            head1 = sb(w, "head1", [P, D])
            fin1 = sb(w, "fin1", [P, ROW])
            with phase() as c:
                s_w, s_t = sem("l1w_loaded"), sem("l1w_turned")
                block = c.enter_context(nc.Block())

                @block.sync
                def _(sp):
                    sp.dma_start(w_raw[:, :], W["L1_gnn_W_attn"]).then_inc(s_w, 16)
                    sp.dma_start(bias1[:, D:2 * D], bc(W["L1_gnn_b_attn"], 0, [P, D])).then_inc(s_w, 16)
                    sp.dma_start(wout[:, :], bc(W["L1_gnn_w_out"], 0, [P, D])).then_inc(s_w, 16)

                @block.tensor
                def _(pe):
                    pe.wait_ge(s_w, 48)
                    pe.transpose(bank[0][0:D, 0:D], w_raw[:, 0:D], ident[0:D, 0:D])
                    pe.transpose(bank[0][0:D, D:2 * D], w_raw[:, D:2 * D], ident[0:D, 0:D]).then_inc(s_t, 1)

                @block.vector
                def _(dve):
                    dve.memset(bias1[:, 0:D], 0.0)
                    dve.wait_ge(s_t, 1)
                    dve.tensor_copy(w_attn[:, :], bank[0][0:D, 0:2 * D])
            with phase() as c:
                tab = sb(c, "tab1", [P, K, ROW + 2 * D])
                project("l1p", x_sb, w_attn[:, :], bias1[:, :], 2 * D, tab, ROW)
                s_row, s_tab, s_hd = (sem(f"l1t_{n}") for n in ("filled", "stored", "rows_stored"))
                s_sc = pool_dma_sem("l1t_scattered")
                block = c.enter_context(nc.Block())

                @block.vector
                def _(dve):
                    dve.memset(tab[:, :, D:ROW], 1.0).then_inc(s_row, 1)
                    dve.tensor_copy(tab[:, :, 0:D], x_sb[:, :, :]).then_inc(s_row, 1)

                @block.sync
                def _(sp):
                    tv = lambda ap: ap.rearrange("(p k) f -> p k f", k=K)
                    sp.dma_start(tv(tabB_d), tab[:, :, ROW + D:ROW + 2 * D]).then_inc(s_hd, 16)
                    sp.wait_ge(s_row, 2)
                    sp.dma_start(tv(tabG_d), tab[:, :, 0:ROW + D]).then_inc(s_tab, 16)
                    sp.wait_ge(s_tab, 16)

                @block.gpsimd
                def _(pool):
                    for k in range(K):
                        pool.indirect_dma_start(
                            out=firstrows_d, out_offset=bass.IndirectOffsetOnAxis(ap=first_i[:, k:k + 1], axis=0),
                            in_=tab[:, k, ROW + D:ROW + 2 * D], in_offset=None,
                            bounds_check=E - 1, oob_is_err=False).then_inc(s_sc, 16)
                    pool.wait_ge(s_hd, 16)
                    pool.indirect_dma_start(
                        out=head1[:, :], out_offset=None, in_=tabB_d,
                        in_offset=bass.IndirectOffsetOnAxis(ap=head_i[:, 0:1], axis=0)).then_inc(s_sc, 16)
                    pool.wait_ge(s_sc, 16 * (K + 1))
            segments("e1", "attn", tabG_d, src_c, head1, wout, fin1)
            with phase() as c:
                S = sb(c, "S1", [P, K, ROW])
                finish_segments("f1", fin1, S)
                sq = sb(c, "sq1", [P, K, D])
                m = sb(c, "m1", [P, K])
                s_var, s_std = sem("n1_var"), sem("n1_std")
                block = c.enter_context(nc.Block())

                @block.scalar
                def _(act):
                    layernorm(None, act, None, None, m, s_var, s_std, "act")

                @block.vector
                def _(dve):
                    step = Steps(dve, sem("order_n1"))
                    step(dve.tensor_tensor(m[:, :], S[:, :, D], nonempty[:, :], ALU.mult))
                    step(dve.scalar_tensor_tensor(m[:, :], m[:, :], 0.0, m[:, :], ALU.is_equal, ALU.add))
                    step(dve.reciprocal(m[:, :], m[:, :]))
                    step(dve.tensor_tensor(m[:, :], m[:, :], nonempty[:, :], ALU.mult))
                    step(dve.tensor_tensor(sq[:, :, :], S[:, :, 0:D], bc(m[:, :], 2, [P, K, D]), ALU.mult))
                    step(dve.tensor_tensor(x_sb[:, :, :], x_sb[:, :, :], sq[:, :, :], ALU.add))
                    layernorm(dve, None, step, sq[:, :, :], m, s_var, s_std, "dve")

        with phase() as w:
            h_mid = sb(w, "h_mid", [P, K, D])
            zero_row = sb(w, "zero_row", [P, D])
            w2c = [sb(w, f"w2c{i}", [D, D]) for i in range(2)]
            rowsw = {n: sb(w, f"row_{n}", [P, D]) for n in ("as1", "ad1", "b1", "as2", "ad2", "b2", "bn_gamma",
                                                             "bn_beta", "bn_mean", "bn_var")}
            with phase() as c:
                s_w, s_s = sem("l2w_loaded"), sem("l2w_sqrt")
                s_v = sem("l2w_var")
                block = c.enter_context(nc.Block())

                @block.sync
                def _(sp):
                    for i in range(2):
                        sp.dma_start(w2c[i][:, :], W[f"L2_gnn_W{i + 1}"]).then_inc(s_w, 16)
                    for n, t in rowsw.items():
                        sp.dma_start(t[:, :], bc(W[f"L2_gnn_{n}"], 0, [P, D])).then_inc(s_w, 16)

                @block.scalar
                def _(act):
                    act.wait_ge(s_v, 1)
                    act.activation(rowsw["bn_var"][:, :], rowsw["bn_var"][:, :], ACT.Sqrt).then_inc(s_s, 1)

                @block.vector
                def _(dve):
                    step = Steps(dve, sem("order_l2w"))
                    g, be, mu, va = (rowsw[f"bn_{n}"][:, :] for n in ("gamma", "beta", "mean", "var"))
                    dve.memset(zero_row[:, :], 0.0)
                    dve.wait_ge(s_w, 16 * 12)
                    dve.tensor_scalar(va, va, BN_EPS, None, ALU.add).then_inc(s_v, 1)
                    dve.wait_ge(s_s, 1)
                    step(dve.reciprocal(va, va))
                    step(dve.tensor_tensor(g, g, va, ALU.mult))
                    step(dve.tensor_tensor(mu, mu, g, ALU.mult))
                    step(dve.tensor_tensor(be, be, mu, ALU.subtract))
            for conv in (1, 2):
                h_in = x_sb if conv == 1 else h_mid
                tg = f"c{conv}"
                with phase() as c:
                    tab = sb(c, f"{tg}_tab", [P, K, ROW])
                    ad = sb(c, f"{tg}_ad", [P, K])
                    fin2 = sb(c, f"{tg}_fin", [P, ROW])
                    head2 = sb(c, f"{tg}_head", [P, 1])
                    project(f"{tg}p", h_in, w2c[conv - 1][:, :], zero_row[:, :], D, tab, 0)
                    with phase() as cc:
                        prod = sb(cc, f"{tg}_prod", [P, K, D])
                        s_row, s_tab, s_hd = (sem(f"{tg}t_{n}") for n in ("filled", "stored", "logits_stored"))
                        s_sc = pool_dma_sem(f"{tg}t_scattered")
                        block = cc.enter_context(nc.Block())

                        @block.vector
                        def _(dve):
                            step = Steps(dve, sem(f"order_{tg}t"))
                            step(dve.memset(tab[:, :, D], 1.0))
                            for name, dest in ((f"ad{conv}", ad[:, :]), (f"as{conv}", tab[:, :, D + 1])):
                                step(dve.tensor_tensor(prod[:, :, :], tab[:, :, 0:D],
                                                       bc(rowsw[name][:, :], 1, [P, K, D]), ALU.mult))
                                step(dve.tensor_reduce(dest, prod[:, :, :], AX, ALU.add))
                            dve.sem_inc(s_row, 1)

                        @block.sync
                        def _(sp):
                            sp.wait_ge(s_row, 1)
                            sp.dma_start(nodes(tabS_d), ad[:, :]).then_inc(s_hd, 16)
                            sp.dma_start(nodes(tabH_d), tab[:, :, :].rearrange("p k f -> p (k f)"))\
                                .then_inc(s_tab, 16)
                            sp.wait_ge(s_tab, 16)

                        @block.gpsimd
                        def _(pool):
                            pool.wait_ge(s_row, 1)
                            for k in range(K):
                                pool.indirect_dma_start(
                                    out=firstad_d,
                                    out_offset=bass.IndirectOffsetOnAxis(ap=first_i[:, k:k + 1], axis=0),
                                    in_=ad[:, k:k + 1], in_offset=None,
                                    bounds_check=E - 1, oob_is_err=False).then_inc(s_sc, 16)
                            pool.wait_ge(s_hd, 16)
                            pool.indirect_dma_start(
                                out=head2[:, :], out_offset=None, in_=tabS_d,
                                in_offset=bass.IndirectOffsetOnAxis(ap=head_i[:, 0:1], axis=0)).then_inc(s_sc, 16)
                            pool.wait_ge(s_sc, 16 * (K + 1))
                    segments(f"{tg}e", "gat", tabH_d, src_c, head2, None, fin2)
                    S = sb(c, f"{tg}_S", [P, K, ROW])
                    finish_segments(f"{tg}f", fin2, S)
                    sq = sb(c, f"{tg}_sq", [P, K, D])
                    m = sb(c, f"{tg}_m", [P, K])
                    own = sb(c, f"{tg}_own", [P, K])
                    top = sb(c, f"{tg}_topn", [P, K])
                    ab = sb(c, f"{tg}_abn", [P, 2, K])
                    s_var, s_std, s_ab, s_eab = (sem(f"{tg}n_{n}") for n in ("var", "std", "offsets", "factors"))
                    block = c.enter_context(nc.Block())

                    @block.scalar
                    def _(act):
                        act.wait_ge(s_ab, 1)
                        act.activation(ab[:, :, :], ab[:, :, :], ACT.Exp).then_inc(s_eab, 1)
                        if conv == 2:
                            layernorm(None, act, None, None, m, s_var, s_std, "act")

                    @block.vector
                    def _(dve):
                        step = Steps(dve, sem(f"order_{tg}n"))
                        step(dve.tensor_tensor(own[:, :], tab[:, :, D + 1], ad[:, :], ALU.add))
                        step(dve.scalar_tensor_tensor(own[:, :], own[:, :], NEG_SLOPE, own[:, :], ALU.mult, ALU.max))
                        step(dve.tensor_scalar(m[:, :], nonempty[:, :], 1.0, BIG, ALU.subtract, ALU.mult))
                        step(dve.tensor_tensor(top[:, :], S[:, :, D + 1], nonempty[:, :], ALU.mult))
                        step(dve.tensor_tensor(m[:, :], m[:, :], top[:, :], ALU.add))
                        step(dve.tensor_tensor(top[:, :], m[:, :], own[:, :], ALU.max))
                        step(dve.tensor_tensor(ab[:, 0, :], own[:, :], top[:, :], ALU.subtract))
                        dve.tensor_tensor(ab[:, 1, :], m[:, :], top[:, :], ALU.subtract).then_inc(s_ab, 1)
                        dve.wait_ge(s_eab, 1)
                        step(dve.tensor_tensor(ab[:, 1, :], ab[:, 1, :], nonempty[:, :], ALU.mult))
                        step(dve.tensor_tensor(m[:, :], S[:, :, D], ab[:, 1, :], ALU.mult))
                        step(dve.tensor_tensor(m[:, :], m[:, :], ab[:, 0, :], ALU.add))
                        step(dve.tensor_scalar(m[:, :], m[:, :], 1e-16, None, ALU.add))
                        step(dve.reciprocal(m[:, :], m[:, :]))
                        step(dve.tensor_tensor(ab[:, :, :], ab[:, :, :], bc(m[:, :], 1, [P, 2, K]), ALU.mult))
                        step(dve.tensor_tensor(sq[:, :, :], S[:, :, 0:D], bc(ab[:, 1, :], 2, [P, K, D]), ALU.mult))
                        step(dve.tensor_tensor(tab[:, :, 0:D], tab[:, :, 0:D], bc(ab[:, 0, :], 2, [P, K, D]),
                                               ALU.mult))
                        step(dve.tensor_tensor(sq[:, :, :], sq[:, :, :], tab[:, :, 0:D], ALU.add))
                        step(dve.tensor_tensor(sq[:, :, :], sq[:, :, :], bc(rowsw[f"b{conv}"][:, :], 1, [P, K, D]),
                                               ALU.add))
                        if conv == 1:
                            step(dve.scalar_tensor_tensor(h_mid[:, :, :], sq[:, :, :], 0.0,
                                                          bc(rowsw["bn_gamma"][:, :], 1, [P, K, D]),
                                                          ALU.max, ALU.mult))
                            step(dve.tensor_tensor(h_mid[:, :, :], h_mid[:, :, :],
                                                   bc(rowsw["bn_beta"][:, :], 1, [P, K, D]), ALU.add))
                        else:
                            step(dve.scalar_tensor_tensor(x_sb[:, :, :], sq[:, :, :], 0.0, x_sb[:, :, :],
                                                          ALU.max, ALU.add))
                            layernorm(dve, None, step, sq[:, :, :], m, s_var, s_std, "dve")

        with phase() as w:
            w3 = sb(w, "w3", [D, R * D])
            w_res = sb(w, "w_res", [D, D])
            rows3 = {n: sb(w, f"row_{n}", [P, D]) for n in ("bias", "res_b", "gamma", "beta")}
            fin3 = sb(w, "fin3", [P, ROW])
            NB = R * D // 512
            with phase() as c:
                comp = sb(c, "comp", [R, R])
                compT = sb(c, "compT", [R, R])
                basis = sb(c, "basis", [R, D * D])
                wr = sb(c, "wr", [R, D * D])
                res_raw = sb(c, "res_raw", [D, D])
                s_w, s_t, s_tc, s_mm, s_wr, s_wrd, s_w3 = (sem(f"l3w_{n}") for n in (
                    "loaded", "turned", "copied", "mixed", "mix_copied", "mix_stored", "mix_loaded"))
                block = c.enter_context(nc.Block())

                @block.sync
                def _(sp):
                    sp.dma_start(comp[:, :], W["L3_gnn_comp"]).then_inc(s_w, 16)
                    sp.dma_start(basis[:, :], W["L3_gnn_basis"].rearrange("b i o -> b (i o)")).then_inc(s_w, 16)
                    sp.dma_start(res_raw[:, :], W["L3_gnn_res_w"]).then_inc(s_w, 16)
                    for n, t in rows3.items():
                        sp.dma_start(t[:, :], bc(W[f"L3_gnn_{n}"], 0, [P, D])).then_inc(s_w, 16)
                    sp.wait_ge(s_w, 16 * 7)
                    sp.wait_ge(s_wr, NB)
                    sp.dma_start(wr_d, wr[:, :]).then_inc(s_wrd, 16)
                    sp.wait_ge(s_wrd, 16)
                    sp.dma_start(w3[:, :].rearrange("i (r o) -> i r o", o=D),
                                 wr_d.rearrange("r (i o) -> i r o", o=D)).then_inc(s_w3, 16)
                    sp.wait_ge(s_w3, 16)

                @block.tensor
                def _(pe):
                    pe.wait_ge(s_w, 16 * 7)
                    pe.transpose(bank[0][0:R, 0:R], comp[:, :], ident[0:R, 0:R])
                    pe.transpose(bank[0][0:D, D:2 * D], res_raw[:, :], ident[0:D, 0:D]).then_inc(s_t, 1)
                    pe.wait_ge(s_tc, 2)
                    for q in range(NB):
                        pe.matmul(bank[q][0:R, :], lhsT=compT[:, :], rhs=basis[:, q * 512:(q + 1) * 512],
                                  start=True, stop=True).then_inc(s_mm, 1)

                @block.vector
                def _(dve):
                    dve.wait_ge(s_t, 1)
                    dve.tensor_copy(compT[:, :], bank[0][0:R, 0:R]).then_inc(s_tc, 1)
                    dve.tensor_copy(w_res[:, :], bank[0][0:D, D:2 * D]).then_inc(s_tc, 1)
                    for q in range(NB):
                        dve.wait_ge(s_mm, q + 1)
                        dve.tensor_copy(wr[:, q * 512:(q + 1) * 512], bank[q][0:R, :]).then_inc(s_wr, 1)

            with phase() as c:
                xc = sb(c, "l3_xc", [P, 2 * D])
                xT = sb(c, "l3_xT", [D, 2 * P])
                yb = [sb(c, f"yb{h}", [P, R * D]) for h in range(2)]
                s_cut, s_t, s_lo, s_hi = (sem(f"l3t_{n}") for n in ("cut", "turned", "low_copied", "high_copied"))
                s_mm = [sem(f"l3t_multiplied{e}") for e in range(2)]
                s_ev = [sem(f"l3t_copied{e}") for e in range(2)]
                s_y = [sem(f"l3t_stored{h}") for h in range(2)]
                xf = x_sb[:, :, :].rearrange("p k f -> p (k f)")
                y_v = y_d.rearrange("(p q) f -> p (q f)", p=P)
                block = c.enter_context(nc.Block())

                def trips(eng, body):
                    body(0)
                    with eng.Fori(1, K // 2) as i:
                        body(i)

                @block.gpsimd
                def _(pool):
                    def body(i):
                        if since(i, 1):
                            hold(pool, s_t, i)
                        pool.tensor_copy(xc[:, :], xf[:, bass.ds(i * (2 * D), 2 * D)]).then_inc(s_cut, 1)
                    trips(pool, body)

                @block.tensor
                def _(pe):
                    def body(i):
                        hold(pe, s_cut, i + 1)
                        pe.transpose(bank[0][:, 0:P], xc[:, :], ident[:, :]).then_inc(s_t, 1)
                        hold(pe, s_lo, i + 1)
                        hold(pe, s_hi, i + 1)
                        for m in range(2 * NB):
                            h, q, e = m // NB, m % NB, m % 2
                            if m >= 4 or since(i, 1):
                                hold(pe, s_ev[e], i * NB + (m // 2 - 1))
                            pe.matmul(bank[1 + m % 4][:, :], lhsT=xT[:, h * P:(h + 1) * P],
                                      rhs=w3[:, q * 512:(q + 1) * 512], start=True, stop=True).then_inc(s_mm[e], 1)
                    trips(pe, body)

                def copies(eng, e, i, copy):
                    for m in range(e, 2 * NB, 2):
                        h, q = m // NB, m % NB
                        if q == e and since(i, 1):
                            hold(eng, s_y[h], i * 16)
                        eng.wait_ge(s_mm[e], i * NB + (m // 2 + 1))
                        copy(yb[h][:, q * 512:(q + 1) * 512], bank[1 + m % 4][:, :]).then_inc(s_ev[e], 1)

                @block.scalar
                def _(act):
                    def body(i):
                        act.wait_ge(s_t, i + 1)
                        act.activation(xT[:, 0:P], bank[0][0:D, 0:P], ACT.Copy).then_inc(s_lo, 1)
                        copies(act, 0, i, lambda o, a: act.activation(o, a, ACT.Copy))
                    trips(act, body)

                @block.vector
                def _(dve):
                    def body(i):
                        dve.wait_ge(s_t, i + 1)
                        dve.tensor_copy(xT[:, P:2 * P], bank[0][D:2 * D, 0:P]).then_inc(s_hi, 1)
                        copies(dve, 1, i, lambda o, a: dve.tensor_copy(o, a))
                    trips(dve, body)

                @block.sync
                def _(sp):
                    def body(i):
                        for h in range(2):
                            for e in range(2):
                                sp.wait_ge(s_ev[e], i * NB + NB // 2 * (h + 1))
                            sp.dma_start(y_v[:, bass.ds(i * (2 * R * D) + h * R * D, R * D)], yb[h][:, :])\
                                .then_inc(s_y[h], 16)
                    trips(sp, body)
                    for h in range(2):
                        sp.wait_ge(s_y[h], 16 * (K // 2))

            segments("e3", "rel", y_d, idx3_d, None, None, fin3)
            with phase() as c:
                S = sb(c, "S3", [P, K, ROW])
                finish_segments("f3", fin3, S)
                res = sb(c, "res3", [P, K, D])
                sq = sb(c, "sq3", [P, K, D])
                m = sb(c, "m3", [P, K])
                part = sb(c, "part3", [P, D])
                mean = sb(c, "mean3", [P, D])
                project("l3p", x_sb, w_res[:, :], rows3["res_b"][:, :], D, res, 0)
                s_var, s_std, s_p, s_tot, s_bv, s_bs = (sem(f"n3_{n}") for n in (
                    "var", "std", "partial", "total", "batch_var", "batch_std"))
                block = c.enter_context(nc.Block())

                @block.tensor
                def _(pe):
                    for v in range(2):
                        pe.wait_ge(s_p, v + 1)
                        pe.matmul(bank[v][:, 0:D], lhsT=ones[:, :], rhs=part[:, :], start=True, stop=True)\
                            .then_inc(s_tot, 1)

                @block.scalar
                def _(act):
                    act.wait_ge(s_bv, 1)
                    act.activation(mean[:, :], mean[:, :], ACT.Sqrt).then_inc(s_bs, 1)
                    layernorm(None, act, None, None, m, s_var, s_std, "act")

                @block.vector
                def _(dve):
                    step = Steps(dve, sem("order_n3"))
                    y = sq[:, :, :]
                    over_nodes = lambda ap: ap.rearrange("p k f -> p f k")
                    step(dve.tensor_tensor(y, S[:, :, 0:D], bc(nonempty[:, :], 2, [P, K, D]), ALU.mult))
                    step(dve.tensor_tensor(y, y, bc(rows3["bias"][:, :], 1, [P, K, D]), ALU.add))
                    step(dve.tensor_scalar(y, y, 0.0, None, ALU.max))
                    step(dve.scalar_tensor_tensor(y, res[:, :, :], 0.0, y, ALU.max, ALU.add))
                    step(dve.tensor_tensor(y, y, bc(real[:, :], 2, [P, K, D]), ALU.mult))
                    dve.tensor_reduce(part[:, :], over_nodes(y), AX, ALU.add).then_inc(s_p, 1)
                    dve.wait_ge(s_tot, 1)
                    step(dve.tensor_scalar(mean[:, :], bank[0][:, 0:D], 1.0 / N, None, ALU.mult))
                    step(dve.tensor_tensor(y, y, bc(mean[:, :], 1, [P, K, D]), ALU.subtract))
                    step(dve.tensor_tensor(y, y, bc(real[:, :], 2, [P, K, D]), ALU.mult))
                    step(dve.tensor_tensor(res[:, :, :], y, y, ALU.mult))
                    dve.tensor_reduce(part[:, :], over_nodes(res[:, :, :]), AX, ALU.add).then_inc(s_p, 1)
                    dve.wait_ge(s_tot, 2)
                    dve.tensor_scalar(mean[:, :], bank[1][:, 0:D], 1.0 / N, BN_EPS, ALU.mult, ALU.add).then_inc(s_bv, 1)
                    dve.wait_ge(s_bs, 1)
                    step(dve.reciprocal(mean[:, :], mean[:, :]))
                    step(dve.tensor_tensor(mean[:, :], mean[:, :], rows3["gamma"][:, :], ALU.mult))
                    step(dve.tensor_tensor(y, y, bc(mean[:, :], 1, [P, K, D]), ALU.mult))
                    step(dve.tensor_tensor(y, y, bc(rows3["beta"][:, :], 1, [P, K, D]), ALU.add))
                    step(dve.tensor_tensor(x_sb[:, :, :], x_sb[:, :, :], y, ALU.add))
                    layernorm(dve, None, step, y, m, s_var, s_std, "dve")
        store_out()


_INS = ["x", "src", "dst", "edge_type_64", "edge_weight1"]
_WEIGHTS = ["L0_gnn_W1", "L0_gnn_b1", "L0_gnn_W2", "L0_gnn_b2", "L0_gnn_Wg", "L0_gnn_bg",
            "L1_gnn_W_attn", "L1_gnn_b_attn", "L1_gnn_w_out",
            "L2_gnn_W1", "L2_gnn_as1", "L2_gnn_ad1", "L2_gnn_b1", "L2_gnn_bn_gamma", "L2_gnn_bn_beta",
            "L2_gnn_bn_mean", "L2_gnn_bn_var", "L2_gnn_W2", "L2_gnn_as2", "L2_gnn_ad2", "L2_gnn_b2",
            "L3_gnn_basis", "L3_gnn_comp", "L3_gnn_bias", "L3_gnn_res_w", "L3_gnn_res_b",
            "L3_gnn_gamma", "L3_gnn_beta"]


def kernel(**inputs):
    import numpy as _np
    import concourse.bacc as _bacc
    from concourse import mybir as _mybir
    from concourse.bass_utils import run_bass_kernel_spmd as _run

    nc = _bacc.Bacc("TRN2", target_bir_lowering=False, num_devices=1)
    arrays, aps = {}, {}
    for name in _INS + _WEIGHTS:
        a = _np.ascontiguousarray(inputs[name])
        arrays[f"in_{name}"] = a
        aps[name] = nc.dram_tensor(f"in_{name}", a.shape, _mybir.dt.from_np(a.dtype), kind="ExternalInput").ap()
    out = nc.dram_tensor("out_0", (N, D), F32, kind="ExternalOutput").ap()
    program(nc, *(aps[n] for n in _INS), {n: aps[n] for n in _WEIGHTS}, out)
    r = _run(nc, [arrays], core_ids=[0])
    return r.results[0]["out_0"]
```

```python
from contextlib import ExitStack, contextmanager

import concourse.bass as bass
from concourse import mybir

F32 = mybir.dt.float32
BF16 = mybir.dt.bfloat16
I32 = mybir.dt.int32
ALU = mybir.AluOpType
ACT = mybir.ActivationFunctionType
AX = mybir.AxisListType.X

P = 128
N = 12500
E = 400000
D = 64
R = 64
K = -(-N // P)
NP = P * K
L = E // P
T = 25
CH = L // T
RING = 3
LAG = 2
HEAD = 5
BIG = 1e30
SKIP = 1000000.0
NSMP = L // T
GRP = 4
GROUPS = [(g, min(GRP, T - g)) for g in range(0, T, GRP)]
NG = len(GROUPS)
ACCS = 5
OUTER = (CH - HEAD) // RING
ROW = D + 2
PART = 16
PARTS = [(k, min(k + PART, K)) for k in range(0, K, PART)]
HALF = PART // 2
HALVES = [(k, min(k + HALF, K)) for k in range(0, K, HALF)]
LN_EPS = 1e-5
BN_EPS = 1e-5
NEG_SLOPE = 0.2


def chunk_loop(eng, body):
    for j in range(HEAD):
        body(j, j % RING, j // RING)
    with eng.Fori(0, OUTER) as i:
        for v in range(RING):
            j = HEAD + v
            body(i * RING + j, j % RING, i + j // RING)


def since(j, first):
    return not isinstance(j, int) or j >= first


class Steps:

    def __init__(self, eng, sem, apart=False):
        self.apart = apart
        self.eng, self.sem, self.base, self.j, self.per, self.k = eng, sem, 0, None, 0, 0

    def chunk(self, j, per):
        if self.j is None:
            self.base += self.k
        self.j, self.per, self.k = j, per, 0

    def end_chunk(self):
        assert self.k == self.per, (self.k, self.per)

    def end_loop(self, chunks):
        self.base, self.j, self.k = self.base + chunks * self.per, None, 0

    def __call__(self, ins):
        self.k += 1
        ins.then_inc(self.sem, 1)
        value = self.base + self.k if self.j is None else self.j * self.per + (self.base + self.k)
        self.eng.wait_ge(self.sem, value)
        if self.apart:
            self.eng.nop(nofuse=True)


def hold(eng, sem, value):
    eng.wait_ge(sem, value)
    eng.nop(nofuse=True)


def bc(ap, axis, shape):
    return ap.unsqueeze(axis).to_broadcast(shape)


def program(nc, x, src, dst, ety, ew, W, out):
    dram = lambda name, shape, dt=F32: nc.dram_tensor(name, shape, dt, kind="Internal").ap()
    start_d = dram("start_d", [NP, 1])
    last_d = dram("last_d", [NP, 1], I32)
    smp_d = dram("smp_d", [P, NSMP])
    idx3_d = dram("idx3_d", [P, L], I32)
    tabA_d = dram("tabA_d", [NP, D])
    tabB_d = dram("tabB_d", [NP, D])
    firstrows_d = dram("firstrows_d", [E, D])
    firstad_d = dram("firstad_d", [E, 1])
    tabG_d = dram("tabG_d", [NP, ROW + D])
    tabH_d = dram("tabH_d", [NP, ROW])
    tabS_d = dram("tabS_d", [NP, 1])
    state_d = dram("state_d", [E, ROW])
    wr_d = dram("wr_d", [R, D * D])
    y_d = dram("y_d", [NP * R, D])
    acc_d = [dram(f"acc{a}_d", [NP + P, D + 1]) for a in range(ACCS)]

    src_c = src.rearrange("(p l) -> p l", p=P)
    dst_c = dst.rearrange("(p l) -> p l", p=P)
    ety_c = ety.rearrange("(p l) -> p l", p=P)
    nodes = lambda ap: ap.rearrange("(p k) f -> p (k f)", k=K)

    ctx = ExitStack()
    with ctx:
        ctx.enter_context(nc.allow_non_contiguous_dma(reason="columns of one element per partition"))

        def sb(c, name, shape, dt=F32):
            return c.enter_context(nc.sbuf_tensor(name, shape, dt))

        scopes = []

        @contextmanager
        def phase():
            with ExitStack() as c:
                scopes.append([])
                yield c
            used = scopes.pop()
            if used:
                nc.clear_and_free_semaphores(used)
                nc.all_engine_barrier()

        def sem(name):
            scopes[-1].append(nc.alloc_semaphore(name))
            return scopes[-1][-1]

        def pool_dma_sem(name):
            return ctx.enter_context(nc.semaphore(name))

        bank = [ctx.enter_context(nc.psum_tensor(f"bank{i}", [P, 512], F32)) for i in range(8)]
        x_sb = sb(ctx, "x_sb", [P, K, D])
        ident = sb(ctx, "ident", [P, P])
        below = sb(ctx, "below", [P, P])
        above = sb(ctx, "above", [P, P])
        ones = sb(ctx, "ones", [P, P])
        cont = sb(ctx, "cont", [P, L])
        nonempty = sb(ctx, "nonempty", [P, K])
        last_i = sb(ctx, "last_i", [P, K], I32)
        first_i = sb(ctx, "first_i", [P, K], I32)
        head_i = sb(ctx, "head_i", [P, 1], I32)
        fix_i = sb(ctx, "fix_i", [P, 1], I32)
        lastq_i = sb(ctx, "lastq_i", [P, 1], I32)
        carryT = sb(ctx, "carryT", [P, P])
        trash = sb(ctx, "trash", [P, 1])
        real = sb(ctx, "real", [P, K])
        acc_landed = [pool_dma_sem(f"acc_landed{a}") for a in range(ACCS)]

        with phase() as c:
            dst_i = sb(c, "dst_i", [P, L], I32)
            dstf = sb(c, "dstf", [P, L])
            prev0_i = sb(c, "prev0_i", [P, 1], I32)
            prev0 = sb(c, "prev0", [P, 1])
            src_i = sb(c, "src_i", [P, L], I32)
            ety_i = sb(c, "ety_i", [P, L], I32)
            zeros = sb(c, "zeros", [P, 6435])
            nid_i = sb(c, "nid_i", [P, K], I32)
            nid = sb(c, "nid", [P, K])
            big = sb(c, "big", [P, K * P])
            smp = sb(c, "smp", [P, NSMP])
            frow = sb(c, "frow", [P, P])
            cnt = sb(c, "cnt", [P, K])
            blk = sb(c, "blk", [P, K])
            blk_i = sb(c, "blk_i", [P, K], I32)
            start = sb(c, "start", [P, K])
            end = sb(c, "end", [P, K])
            tmp = sb(c, "tmp", [P, K])
            hi_i = sb(c, "hi_i", [P, 1], I32)
            hi = sb(c, "hi", [P, 1])
            lastq = sb(c, "lastq", [P, 1])
            valid = sb(c, "valid", [P, 1])
            trash_i = sb(c, "trash_i", [P, 1], I32)
            s_x0, s_x, s_dst, s_src, s_zero, s_iota, s_mask = (sem(n) for n in (
                "x_cleared", "x_loaded", "dst_loaded", "src_loaded", "zeros_set", "iota_done", "mask_done"))
            s_cast, s_row, s_rowc, s_smp, s_smpd = (sem(n) for n in (
                "dst_cast", "row_spread", "row_copied", "samples_cut", "samples_stored"))
            s_b1, s_b2, s_st, s_std, s_en, s_la, s_lad, s_i3, s_i3d = (sem(n) for n in (
                "block_found", "run_found", "start_found", "start_stored", "end_loaded", "last_found",
                "last_stored", "idx3_made", "idx3_stored"))
            s_fill = [sem(f"firstrows_cleared{b}") for b in range(2)]
            s_g1, s_g2, s_lq = (pool_dma_sem(n) for n in ("samples_gathered", "runs_gathered", "lastq_gathered"))
            block = c.enter_context(nc.Block())

            @block.sync
            def _(sp):
                sp.dma_start(dst_i[:, :], dst_c).then_inc(s_dst, 16)
                sp.wait_ge(s_iota, 1)
                sp.dma_start(prev0_i[1:P, :], dst_c[0:P - 1, L - 1:L]).then_inc(s_dst, 16)
                sp.dma_start(src_i[:, :], src_c).then_inc(s_src, 16)
                sp.dma_start(ety_i[:, :], ety_c).then_inc(s_src, 16)
                sp.wait_ge(s_smp, 1)
                sp.dma_start(smp_d[:, :], smp[:, :]).then_inc(s_smpd, 16)
                sp.wait_ge(s_i3, 1)
                sp.dma_start(idx3_d[:, :], src_i[:, :]).then_inc(s_i3d, 16)
                sp.wait_ge(s_st, 1)
                sp.dma_start(start_d.rearrange("(p k) f -> p (k f)", k=K), start[:, :]).then_inc(s_std, 16)
                sp.wait_ge(s_std, 16)
                sp.dma_start(end[0:P - 1, K - 1:K], start_d.rearrange("(p k) f -> p (k f)", k=K)[1:P, 0:1])\
                    .then_inc(s_en, 16)
                sp.wait_ge(s_la, 1)
                sp.dma_start(nodes(last_d), last_i[:, :]).then_inc(s_lad, 16)
                sp.wait_ge(s_i3d, 16)

            @block.scalar
            def _(act):
                xv = x_sb[:, :, :].rearrange("p k f -> p (k f)")
                rows = lambda a, b: x[a * K:b * K, :].rearrange("(p k) f -> p (k f)", k=K)
                act.wait_ge(s_x0, 1)
                act.dma_start(xv[0:96, :], rows(0, 96)).then_inc(s_x, 16)
                act.dma_start(xv[96:126, :], rows(96, 126)).then_inc(s_x, 16)
                act.dma_start(xv[126:127, :], rows(126, 127)).then_inc(s_x, 16)
                rest = N - 127 * K
                act.dma_start(xv[127:128, 0:rest * D],
                              x[127 * K:N, :].rearrange("(p k) f -> p (k f)", k=rest)).then_inc(s_x, 16)
                act.wait_ge(s_zero, 1)
                fr = firstrows_d.rearrange("(p l) f -> p (l f)", p=P)
                for b in range(32):
                    act.dma_start(fr[:, b * 6250:(b + 1) * 6250], zeros[:, 0:6250]).then_inc(s_fill[b % 2], 16)
                    if b >= 1:
                        act.wait_ge(s_fill[(b - 1) % 2], ((b - 1) // 2 + 1) * 16)
                act.wait_ge(s_fill[1], 16 * 16)
                act.dma_start(firstad_d.rearrange("(p l) f -> p (l f)", p=P), zeros[:, 0:L]).then_inc(s_fill[0], 16)
                act.wait_ge(s_fill[0], 17 * 16)
                act.wait_ge(s_x, 64)

            @block.gpsimd
            def _(pool):
                step = Steps(pool, s_mask)
                pool.iota(nid_i[:, :], [[1, K]], base=0, channel_multiplier=K)
                pool.iota(hi_i[:, :], [[0, 1]], base=L, channel_multiplier=L)
                pool.iota(trash_i[:, :], [[0, 1]], base=NP, channel_multiplier=1)
                pool.memset(prev0_i[:, :], -1).then_inc(s_iota, 1)
                step(pool.memset(ident[:, :], 0.0))
                step(pool.memset(below[:, :], 1.0))
                step(pool.memset(above[:, :], 1.0))
                step(pool.memset(ones[:, :], 1.0))
                step(pool.affine_select(out=ident[:, :], in_=ident[:, :], compare_op=ALU.not_equal, fill=1.0,
                                        base=0, pattern=[[-1, P]], channel_multiplier=1))
                step(pool.affine_select(out=below[:, :], in_=below[:, :], compare_op=ALU.is_gt, fill=0.0,
                                        base=0, pattern=[[-1, P]], channel_multiplier=1))
                step(pool.affine_select(out=above[:, :], in_=above[:, :], compare_op=ALU.is_gt, fill=0.0,
                                        base=0, pattern=[[1, P]], channel_multiplier=-1))
                pool.wait_ge(s_zero, 1)
                for a in range(ACCS):
                    pool.dma_start(acc_d[a].rearrange("(p q) f -> p (q f)", p=P), zeros[:, :])\
                        .then_inc(acc_landed[a], 16)
                pool.wait_ge(s_smpd, 16)
                pool.wait_ge(s_b1, 1)
                for k in range(K):
                    pool.indirect_dma_start(
                        out=big[:, k * NSMP:(k + 1) * NSMP], out_offset=None, in_=smp_d,
                        in_offset=bass.IndirectOffsetOnAxis(ap=blk_i[:, k:k + 1], axis=0)).then_inc(s_g1, 16)
                pool.wait_ge(s_b2, 1)
                runs = dst.rearrange("(a b) -> a b", b=T)
                bigi = big[:, :].bitcast(I32)
                for k in range(K):
                    pool.indirect_dma_start(
                        out=bigi[:, k * T:(k + 1) * T], out_offset=None, in_=runs,
                        in_offset=bass.IndirectOffsetOnAxis(ap=blk_i[:, k:k + 1], axis=0)).then_inc(s_g2, 16)
                pool.wait_ge(s_lad, 16)
                pool.indirect_dma_start(
                    out=lastq_i[:, :], out_offset=None, in_=last_d,
                    in_offset=bass.IndirectOffsetOnAxis(ap=dst_i[:, 0:1], axis=0)).then_inc(s_lq, 16)
                for a in range(ACCS):
                    pool.wait_ge(acc_landed[a], 16)

            @block.tensor
            def _(pe):
                pe.wait_ge(s_cast, 1)
                pe.wait_ge(s_mask, 7)
                pe.matmul(bank[0][:, 0:P], lhsT=dstf[:, 0:1].to_broadcast([P, P]), rhs=ident[:, :],
                          start=True, stop=True)
                pe.matmul(bank[1][:, 0:P], lhsT=dstf[:, L - 1:L].to_broadcast([P, P]), rhs=ident[:, :],
                          start=True, stop=True).then_inc(s_row, 1)

            @block.vector
            def _(dve):
                step = Steps(dve, sem("order_setup"))
                dve.memset(x_sb[:, :, :], 0.0).then_inc(s_x0, 1)
                dve.memset(zeros[:, :], 0.0).then_inc(s_zero, 1)
                dve.wait_ge(s_dst, 32)
                step(dve.tensor_copy(dstf[:, :], dst_i[:, :]))
                step(dve.tensor_copy(smp[:, :], dstf[:, 0:L:T]))
                dve.tensor_copy(prev0[:, :], prev0_i[:, :]).then_inc(s_smp, 1)
                dve.tensor_copy(head_i[:, :], dst_i[:, 0:1]).then_inc(s_cast, 1)
                dve.wait_ge(s_smp, 1)
                dve.wait_ge(s_iota, 1)
                step(dve.tensor_tensor(cont[:, 1:L], dstf[:, 1:L], dstf[:, 0:L - 1], ALU.is_equal))
                step(dve.tensor_tensor(cont[:, 0:1], dstf[:, 0:1], prev0[:, :], ALU.is_equal))
                step(dve.tensor_copy(nid[:, :], nid_i[:, :]))
                step(dve.tensor_scalar(real[:, :], nid[:, :], float(N), None, ALU.is_lt))
                step(dve.tensor_copy(hi[:, :], hi_i[:, :]))
                step(dve.tensor_copy(trash[:, :], trash_i[:, :]))
                dve.wait_ge(s_row, 1)
                step(dve.tensor_copy(frow[:, :], bank[0][:, 0:P]))
                cmp1 = big[:, :].rearrange("p (k q) -> p k q", q=P)
                step(dve.tensor_tensor(cmp1, bc(frow[:, :], 1, [P, K, P]), bc(nid[:, :], 2, [P, K, P]), ALU.is_lt))
                step(dve.tensor_reduce(cnt[:, :], cmp1, AX, ALU.add))
                step(dve.tensor_scalar(blk[:, :], cnt[:, :], 1.0, 0.0, ALU.subtract, ALU.max))
                dve.tensor_copy(blk_i[:, :], blk[:, :]).then_inc(s_b1, 1)
                dve.wait_ge(s_g1, 16 * K)
                smps = big[:, 0:K * NSMP].rearrange("p (k q) -> p k q", q=NSMP)
                step(dve.tensor_tensor(smps, smps, bc(nid[:, :], 2, [P, K, NSMP]), ALU.is_lt))
                step(dve.tensor_reduce(cnt[:, :], smps, AX, ALU.add))
                step(dve.tensor_scalar(cnt[:, :], cnt[:, :], 1.0, 0.0, ALU.subtract, ALU.max))
                step(dve.scalar_tensor_tensor(blk[:, :], blk[:, :], float(NSMP), cnt[:, :], ALU.mult, ALU.add))
                dve.tensor_copy(blk_i[:, :], blk[:, :]).then_inc(s_b2, 1)
                step(dve.scalar_tensor_tensor(carryT[:, :], bank[1][:, 0:P], dstf[:, 0:1], below[:, :],
                                              ALU.is_equal, ALU.mult))
                dve.wait_ge(s_src, 32)
                dve.scalar_tensor_tensor(src_i[:, :], src_i[:, :], float(R), ety_i[:, :], ALU.mult, ALU.add)\
                    .then_inc(s_i3, 1)
                dve.wait_ge(s_g2, 16 * K)
                runs = big[:, 0:K * T].bitcast(I32).rearrange("p (k q) -> p k q", q=T)
                lt = big[:, K * T:2 * K * T].rearrange("p (k q) -> p k q", q=T)
                step(dve.tensor_copy(lt, runs))
                step(dve.tensor_tensor(lt, lt, bc(nid[:, :], 2, [P, K, T]), ALU.is_lt))
                step(dve.tensor_reduce(cnt[:, :], lt, AX, ALU.add))
                step(dve.scalar_tensor_tensor(start[:, :], blk[:, :], float(T), cnt[:, :], ALU.mult, ALU.add))
                step(dve.memset(end[:, K - 1:K], float(E)))
                dve.tensor_copy(end[:, 0:K - 1], start[:, 1:K]).then_inc(s_st, 1)
                dve.wait_ge(s_en, 16)
                dve.wait_ge(s_st, 1)
                step(dve.tensor_tensor(nonempty[:, :], end[:, :], start[:, :], ALU.is_gt))
                step(dve.tensor_scalar(end[:, :], end[:, :], 1.0, 0.0, ALU.subtract, ALU.max))
                dve.tensor_copy(last_i[:, :], end[:, :]).then_inc(s_la, 1)
                step(dve.tensor_scalar(tmp[:, :], nonempty[:, :], -SKIP, SKIP, ALU.mult, ALU.add))
                step(dve.tensor_tensor(tmp[:, :], tmp[:, :], start[:, :], ALU.add))
                step(dve.tensor_copy(first_i[:, :], tmp[:, :]))
                dve.wait_ge(s_lq, 16)
                step(dve.tensor_copy(lastq[:, :], lastq_i[:, :]))
                step(dve.tensor_tensor(valid[:, :], lastq[:, :], hi[:, :], ALU.is_lt))
                step(dve.tensor_scalar(valid[:, :], valid[:, :], -SKIP, SKIP, ALU.mult, ALU.add))
                step(dve.tensor_tensor(lastq[:, :], lastq[:, :], valid[:, :], ALU.add))
                step(dve.tensor_copy(fix_i[:, :], lastq[:, :]))

        def projection(tag, c, h_in, w, bias, cols, tab, off):
            xT = [sb(c, f"{tag}_xT{b}", [D, 2, HALF // 2 * P]) for b in range(2)]
            s_t, s_cp, s_mm, s_o = (sem(f"{tag}_{n}") for n in ("turned", "turn_copied", "multiplied", "put"))
            per_bank = 512 // cols

            def turn(pe, g):
                k0, k1 = HALVES[g]
                if g >= 2:
                    pe.wait_ge(s_cp, g - 1)
                for u in range((k1 - k0) // 2):
                    last = pe.transpose(bank[g % 2][:, u * P:(u + 1) * P],
                                        h_in[:, k0 + 2 * u:k0 + 2 * u + 2, :].rearrange("p k f -> p (k f)"),
                                        ident[:, :])
                last.then_inc(s_t, 1)

            def copy(act, g):
                k0, k1 = HALVES[g]
                n = (k1 - k0) // 2 * P
                act.wait_ge(s_t, g + 1)
                if g >= 2:
                    act.wait_ge(s_mm, g - 1)
                act.activation(xT[g % 2][:, 0, 0:n], bank[g % 2][0:D, 0:n], ACT.Copy)
                act.activation(xT[g % 2][:, 1, 0:n], bank[g % 2][D:2 * D, 0:n], ACT.Copy).then_inc(s_cp, 1)

            def multiply(pe, g):
                k0, k1 = HALVES[g]
                pe.wait_ge(s_cp, g + 1)
                if g >= 2:
                    pe.wait_ge(s_o, g - 1)
                for k in range(k1 - k0):
                    o = bank[2 + 2 * (g % 2) + k // per_bank]
                    last = pe.matmul(o[:, k % per_bank * cols:(k % per_bank + 1) * cols],
                                     lhsT=xT[g % 2][:, k % 2, k // 2 * P:(k // 2 + 1) * P], rhs=w,
                                     start=True, stop=True)
                last.then_inc(s_mm, 1)

            def put(dve, step, g):
                k0, k1 = HALVES[g]
                dve.wait_ge(s_mm, g + 1)
                for n, k in enumerate(range(k0, k1, per_bank)):
                    m = min(per_bank, k1 - k)
                    ps = bank[2 + 2 * (g % 2) + n][:, 0:m * cols].rearrange("p (k f) -> p k f", k=m)
                    step(dve.tensor_tensor(tab[:, k:k + m, off:off + cols], ps, bc(bias, 1, [P, m, cols]), ALU.add))

            return turn, copy, multiply, put, s_o

        def halves(q):
            return [g for g, (k, _) in enumerate(HALVES) if PARTS[q][0] <= k < PARTS[q][1]]

        def node_block(tag, collect=None, load=None, update=None, act_update=None, norm=False, proj=None):
            with phase() as c:
                m = sb(c, f"{tag}_m", [P, K])
                sq = sb(c, f"{tag}_sq", [P, PART, D])
                s_all = [pool_dma_sem(f"{tag}_collected{q}") for q in range(len(PARTS))] if collect is not None else None
                s_x, s_cen, s_sq, s_var, s_std, s_tab = (sem(f"{tag}_{n}") for n in (
                    "updated", "centred", "squared", "var_done", "std_done", "table_stored"))
                if proj:
                    turn, copy, multiply, put, s_o = projection(tag, c, *proj["of"])
                    s_sc = pool_dma_sem(f"{tag}_scattered")
                block = c.enter_context(nc.Block())

                @block.gpsimd
                def _(pool):
                    if collect is not None:
                        for q, (k0, k1) in enumerate(PARTS):
                            for k in range(k0, k1):
                                pool.indirect_dma_start(
                                    out=collect[:, k, :], out_offset=None, in_=state_d,
                                    in_offset=bass.IndirectOffsetOnAxis(ap=last_i[:, k:k + 1], axis=0))\
                                    .then_inc(s_all[q], 16)
                    if proj:
                        target, source = proj["scatter"]
                        for g, (k0, k1) in enumerate(HALVES):
                            pool.wait_ge(s_o, g + 1)
                            for k in range(k0, k1):
                                pool.indirect_dma_start(
                                    out=target, out_offset=bass.IndirectOffsetOnAxis(ap=first_i[:, k:k + 1], axis=0),
                                    in_=source(k), in_offset=None,
                                    bounds_check=E - 1, oob_is_err=False).then_inc(s_sc, 16)
                        pool.wait_ge(s_tab, 16 * len(proj["stores"]) * len(HALVES))
                        head, head_table = proj["head"]
                        pool.indirect_dma_start(
                            out=head[:, :], out_offset=None, in_=head_table,
                            in_offset=bass.IndirectOffsetOnAxis(ap=head_i[:, 0:1], axis=0)).then_inc(s_sc, 16)
                        pool.wait_ge(s_sc, 16 * (K + 1))

                @block.sync
                def _(sp):
                    def store(q):
                        if proj:
                            for g in halves(q):
                                k0, k1 = HALVES[g]
                                sp.wait_ge(s_o, g + 1)
                                for dest, a, b in proj["stores"]:
                                    sp.dma_start(dest.rearrange("(p k) f -> p k f", k=K)[:, k0:k1, :],
                                                 proj["of"][4][:, k0:k1, a:b]
                                                 if a is not None else b[:, k0:k1].unsqueeze(2)).then_inc(s_tab, 16)

                    for q in range(len(PARTS) + 2):
                        if load and q < len(PARTS):
                            if q >= 2:
                                sp.wait_ge(s_x, q - 1)
                            load(sp, q)
                        if q >= 2:
                            store(q - 2)
                    if proj:
                        sp.wait_ge(s_tab, 16 * len(proj["stores"]) * len(HALVES))

                @block.tensor
                def _(pe):
                    if proj:
                        for q in range(len(PARTS)):
                            pe.wait_ge(s_x, q + 1)
                            for g in halves(q):
                                turn(pe, g)
                            for g in halves(q):
                                multiply(pe, g)

                @block.scalar
                def _(act):
                    for q, (k0, k1) in enumerate(PARTS):
                        if act_update:
                            act_update(act, q, k0, k1)
                        if norm:
                            act.wait_ge(s_cen, q + 1)
                            act.activation(sq[:, 0:k1 - k0, :], x_sb[:, k0:k1, :], ACT.Square).then_inc(s_sq, 1)
                            act.wait_ge(s_var, q + 1)
                            act.activation(m[:, k0:k1], m[:, k0:k1], ACT.Sqrt).then_inc(s_std, 1)
                        if proj:
                            for g in halves(q):
                                copy(act, g)

                @block.vector
                def _(dve):
                    step = Steps(dve, sem(f"order_{tag}"))

                    def put_part(q):
                        if proj and q >= 0:
                            for g in halves(q):
                                put(dve, step, g)
                                if "extra" in proj:
                                    proj["extra"](dve, step, *HALVES[g])
                                dve.sem_inc(s_o, 1)

                    for q, (k0, k1) in enumerate(PARTS):
                        xq, mq = x_sb[:, k0:k1, :], m[:, k0:k1]
                        wide = [P, k1 - k0, D]
                        if collect is not None:
                            dve.wait_ge(s_all[q], 16 * (k1 - k0))
                        if update:
                            update(dve, step, q, k0, k1)
                        if norm:
                            step(dve.tensor_reduce(mq, xq, AX, ALU.add))
                            step(dve.tensor_scalar(mq, mq, 1.0 / D, None, ALU.mult))
                            dve.tensor_tensor(xq, xq, bc(mq, 2, wide), ALU.subtract).then_inc(s_cen, 1)
                            put_part(q - 1)
                            dve.wait_ge(s_cen, q + 1)
                            dve.wait_ge(s_sq, q + 1)
                            step(dve.tensor_reduce(mq, sq[:, 0:k1 - k0, :], AX, ALU.add))
                            dve.tensor_scalar(mq, mq, 1.0 / D, LN_EPS, ALU.mult, ALU.add).then_inc(s_var, 1)
                            dve.wait_ge(s_std, q + 1)
                            step(dve.reciprocal(mq, mq))
                            step(dve.tensor_tensor(xq, xq, bc(mq, 2, wide), ALU.mult))
                        else:
                            put_part(q - 1)
                        dve.sem_inc(s_x, 1)
                    put_part(len(PARTS) - 1)

        def layernorm(dve, act, step, sq, m, s_var, s_std, part):
            if part == "act":
                act.wait_ge(s_var, 1)
                act.activation(m[:, :], m[:, :], ACT.Sqrt).then_inc(s_std, 1)
                return
            step(dve.tensor_reduce(m[:, :], x_sb[:, :, :], AX, ALU.add))
            step(dve.tensor_scalar(m[:, :], m[:, :], 1.0 / D, None, ALU.mult))
            step(dve.tensor_tensor(x_sb[:, :, :], x_sb[:, :, :], bc(m[:, :], 2, [P, K, D]), ALU.subtract))
            step(dve.tensor_tensor(sq, x_sb[:, :, :], x_sb[:, :, :], ALU.mult))
            step(dve.tensor_reduce(m[:, :], sq, AX, ALU.add))
            dve.tensor_scalar(m[:, :], m[:, :], 1.0 / D, LN_EPS, ALU.mult, ALU.add).then_inc(s_var, 1)
            dve.wait_ge(s_std, 1)
            step(dve.reciprocal(m[:, :], m[:, :]))
            step(dve.tensor_tensor(x_sb[:, :, :], x_sb[:, :, :], bc(m[:, :], 2, [P, K, D]), ALU.mult))

        w0 = ExitStack()
        w_pair = sb(w0, "w_pair", [D, 2 * D + 2 * D])
        w_ig = sb(w0, "w_ig", [D, 2 * D])
        bias_ig = sb(w0, "bias_ig", [1, GRP, 2 * D])
        bias_pair = sb(w0, "bias_pair", [P, 2 * D])
        with phase() as c:
            wg = sb(c, "wg", [D, D])
            w2T = sb(c, "w2T", [D, D])
            b2c = sb(c, "b2c", [D, 1])
            b2r = sb(c, "b2r", [1, 2 * D])
            s_w, s_bz, s_t, s_tc, s_g = (sem(f"l0w_{n}") for n in ("loaded", "cleared", "turned", "copied", "product"))
            block = c.enter_context(nc.Block())

            @block.sync
            def _(sp):
                sp.dma_start(w_pair[:, 0:D], W["L0_gnn_W1"][0:D, :]).then_inc(s_w, 16)
                sp.dma_start(w_pair[:, D:2 * D], W["L0_gnn_W1"][D:2 * D, :]).then_inc(s_w, 16)
                sp.dma_start(w_ig[:, 0:D], W["L0_gnn_W2"]).then_inc(s_w, 16)
                sp.dma_start(wg[:, :], W["L0_gnn_Wg"]).then_inc(s_w, 16)
                sp.dma_start(b2c[:, :], W["L0_gnn_b2"].unsqueeze(1)).then_inc(s_w, 16)
                sp.dma_start(b2r[:, 0:D], W["L0_gnn_b2"].unsqueeze(0)).then_inc(s_w, 16)
                sp.dma_start(b2r[:, D:2 * D], W["L0_gnn_bg"].unsqueeze(0)).then_inc(s_w, 16)
                sp.dma_start(bias_pair[:, D:2 * D], bc(W["L0_gnn_b1"], 0, [P, D])).then_inc(s_w, 16)

            @block.tensor
            def _(pe):
                pe.wait_ge(s_w, 128)
                pe.transpose(bank[0][0:D, 0:D], w_ig[:, 0:D], ident[0:D, 0:D]).then_inc(s_t, 1)
                pe.matmul(bank[1][0:1, 0:D], lhsT=b2c[:, :], rhs=wg[:, :], start=True, stop=True).then_inc(s_t, 1)
                pe.wait_ge(s_tc, 1)
                pe.matmul(bank[2][0:D, 0:D], lhsT=w2T[:, :], rhs=wg[:, :], start=True, stop=True).then_inc(s_g, 1)

            @block.vector
            def _(dve):
                step = Steps(dve, sem("order_l0w"))
                step(dve.memset(bias_pair[:, 0:D], 0.0))
                dve.wait_ge(s_w, 128)
                dve.wait_ge(s_t, 2)
                dve.tensor_copy(w2T[:, :], bank[0][0:D, 0:D]).then_inc(s_tc, 1)
                step(dve.tensor_tensor(b2r[:, D:2 * D], b2r[:, D:2 * D], bank[1][0:1, 0:D], ALU.add))
                for g in range(GRP):
                    dve.tensor_copy(bias_ig[:, g, :], b2r[:, :])
                dve.wait_ge(s_g, 1)
                step(dve.tensor_copy(w_ig[:, D:2 * D], bank[2][0:D, 0:D]))

        head0 = sb(w0, "head0", [P, D])
        with phase() as c:
            tab = sb(c, "tab0", [P, K, 2 * D])
            node_block("pair", proj={
                "of": (x_sb, w_pair[:, 0:2 * D], bias_pair[:, :], 2 * D, tab, 0),
                "stores": [(tabB_d, D, 2 * D), (tabA_d, 0, D)],
                "scatter": (firstrows_d, lambda k: tab[:, k, D:2 * D]), "head": (head0, tabB_d)})

        with phase() as c:
            idx = [sb(c, f"idx{r}", [P, T], I32) for r in range(RING)]
            G = [sb(c, f"G{r}", [P, T, D]) for r in range(RING)]
            Br = [sb(c, f"Br{r}", [P, T, D]) for r in range(RING)]
            sums = [sb(c, f"sums{r}", [P, T, D + 1]) for r in range(RING)]
            idxs = [sb(c, f"idxs{r}", [P, T], I32) for r in range(RING)]
            srcf = sb(c, "srcf", [P, T])
            contc = sb(c, "contc", [P, T])
            keep = sb(c, "keep", [P, D, T])
            BT = sb(c, "BT", [P, D, T])
            F = sb(c, "F", [P, D, T])
            H = sb(c, "H", [P, T, D])
            HT = sb(c, "HT", [D, GRP * P])
            gate = sb(c, "gate", [P, GRP, D])
            msg = [sb(c, f"msg{b}", [P, GRP, D + 1]) for b in range(2)]
            same = [sb(c, f"same{b}", [P, GRP, P]) for b in range(2)]
            earlier = sb(c, "earlier", [P, GRP, P])
            dup = sb(c, "dup", [P, T])
            to = sb(c, "to", [P, T])
            s_idx = [sem(f"e0_idx{r}") for r in range(RING)]
            s_g = [pool_dma_sem(f"e0_gathered{r}") for r in range(RING)]
            s_br = [sem(f"e0_first_rows{r}") for r in range(RING)]
            (s_brf, s_bt, s_F, s_H, s_T, s_HT, s_I, s_sg, s_B, s_eq, s_C, s_Co, s_to, s_ini) = (
                sem(f"e0_{n}") for n in (
                    "first_rows_free", "first_rows_turned", "filled", "added", "turned", "relu_done",
                    "interaction", "gate_done", "sources_spread", "message_done", "combined", "combined_copied",
                    "targets_done", "started"))
            block = c.enter_context(nc.Block())
            first_v = firstrows_d.rearrange("(p l) f -> p (l f)", p=P)

            @block.sync
            def _(sp):
                def body(j, r, n):
                    sp.wait_ge(s_to, j + 1)
                    sp.dma_start(idx[r][:, :], src_c[:, bass.ds(j * T, T)]).then_inc(s_idx[r], 16)
                    sp.wait_ge(s_brf, j + 1)
                    sp.dma_start(Br[r][:, :, :].rearrange("p t f -> p (t f)"),
                                 first_v[:, bass.ds(j * (T * D), T * D)]).then_inc(s_br[r], 16)
                chunk_loop(sp, body)

            @block.gpsimd
            def _(pool):
                def gather(j, r, n, t):
                    pool.indirect_dma_start(
                        out=G[r][:, t, :], out_offset=None, in_=tabA_d,
                        in_offset=bass.IndirectOffsetOnAxis(ap=idx[r][:, t:t + 1], axis=0)).then_inc(s_g[r], 16)

                def scatter(j, r, t):
                    hold(pool, acc_landed[t % ACCS], j * (16 * T // ACCS) + 16 * (1 + t // ACCS))
                    pool.indirect_dma_start(
                        out=acc_d[t % ACCS], out_offset=bass.IndirectOffsetOnAxis(ap=idxs[r][:, t:t + 1], axis=0),
                        in_=sums[r][:, t, :], in_offset=None, compute_op=ALU.add).then_inc(acc_landed[t % ACCS], 16)

                def ready(j):
                    hold(pool, s_to, j + (1 + RING))
                    hold(pool, s_Co, j * NG + (NG + 2))

                def body(j, r, n):
                    pool.wait_ge(s_idx[r], n * 16 + 16)
                    hold(pool, s_H, j + 1)
                    if since(j, LAG):
                        ready(j - LAG)
                    for t in range(T):
                        gather(j, r, n, t)
                        if since(j, LAG):
                            scatter(j - LAG, (r - LAG) % RING, t)
                chunk_loop(pool, body)
                for j in range(CH - LAG, CH):
                    ready(j)
                    for t in range(T):
                        scatter(j, j % RING, t)
                for a in range(ACCS):
                    pool.wait_ge(acc_landed[a], 16 * (1 + CH * T // ACCS))

            @block.scalar
            def _(act):
                act.sem_inc(s_brf, RING)
                act.sem_inc(s_Co, 2)
                act.wait_ge(s_ini, 1)

                def relu(j, g):
                    n = GROUPS[g][1] * P
                    act.wait_ge(s_T, j * NG + (g + 1))
                    act.activation(HT[:, 0:n], bank[0][0:D, 0:n], ACT.Relu).then_inc(s_HT, 1)

                def body(j, r, n):
                    act.wait_ge(s_br[r], n * 16 + 16)
                    hold(act, s_F, j + 1)
                    act.activation(BT[:, :, :].rearrange("p f t -> p t f"), Br[r][:, :, :], ACT.Copy).then_inc(s_brf, 1)
                    act.activation(keep[:, :, 1:T],
                                   bc(cont[:, bass.ds(j * T + 1, T - 1)], 1, [P, D, T - 1]), ACT.Copy).then_inc(s_bt, 1)
                    relu(j, 0)
                    for g, (t0, m) in enumerate(GROUPS):
                        act.wait_ge(s_I, j * NG + (g + 1))
                        psI = bank[1][:, 0:m * 2 * D].rearrange("p (t f) -> p t f", t=m)
                        act.activation(gate[:, 0:m, :], psI[:, :, D:2 * D], ACT.Sigmoid).then_inc(s_sg, 1)
                        if g + 1 < NG:
                            relu(j, g + 1)
                        act.wait_ge(s_C, j * NG + (g + 1))
                        if g == 0 and since(j, RING):
                            for a in range(ACCS):
                                act.wait_ge(acc_landed[a], (j - (RING - 1)) * (16 * T // ACCS) + 16)
                        psC = bank[4 + g % 2][:, 0:m * (D + 1)].rearrange("p (t f) -> p t f", t=m)
                        act.activation(sums[r][:, t0:t0 + m, :], psC, ACT.Copy).then_inc(s_Co, 1)
                chunk_loop(act, body)

            @block.tensor
            def _(pe):
                def turn(j, g):
                    t0, m = GROUPS[g]
                    for t in range(m):
                        last = pe.transpose(bank[0][0:D, t * P:(t + 1) * P], H[:, t0 + t, :], ident[:, :])
                    last.then_inc(s_T, 1)
                    for t in range(m):
                        last = pe.matmul(bank[2 + g % 2][:, t * P:(t + 1) * P],
                                         lhsT=srcf[:, t0 + t:t0 + t + 1].to_broadcast([P, P]), rhs=ident[:, :],
                                         start=True, stop=True)
                    last.then_inc(s_B, 1)

                def body(j, r, n):
                    hold(pe, s_H, j + (1 + RING))
                    turn(j, 0)
                    for g, (t0, m) in enumerate(GROUPS):
                        hold(pe, s_HT, j * NG + (g + 1))
                        pe.matmul(bank[1][:, 0:m * 2 * D], lhsT=ones[0:1, :],
                                  rhs=bias_ig[:, 0:m, :].rearrange("p t f -> p (t f)"), start=True, stop=False)
                        for t in range(m):
                            last = pe.matmul(bank[1][:, t * 2 * D:(t + 1) * 2 * D], lhsT=HT[:, t * P:(t + 1) * P],
                                             rhs=w_ig[:, :], start=False, stop=(t == m - 1))
                        last.then_inc(s_I, 1)
                        if g + 1 < NG:
                            turn(j, g + 1)
                        hold(pe, s_eq, j * NG + (g + 1))
                        hold(pe, s_Co, j * NG + (g + 1))
                        for t in range(m):
                            last = pe.matmul(bank[4 + g % 2][:, t * (D + 1):(t + 1) * (D + 1)],
                                             lhsT=same[g % 2][:, t, :], rhs=msg[g % 2][:, t, :],
                                             start=True, stop=True)
                        last.then_inc(s_C, 1)
                chunk_loop(pe, body)

            @block.vector
            def _(dve):
                step = Steps(dve, sem("order_e0"))
                dve.sem_inc(s_H, RING)
                dve.sem_inc(s_to, RING)
                step(dve.memset(F[:, :, :], 0.0))
                step(dve.tensor_copy(F[:, :, T - 1], head0[:, :]))
                for b in range(2):
                    step(dve.memset(msg[b][:, :, :], 1.0))
                dve.memset(keep[:, :, :], 0.0).then_inc(s_ini, 1)
                dve.sem_inc(s_F, 1)

                def body(j, r, n):
                    step.chunk(j, 7 + 2 * NG)
                    dve.wait_ge(s_idx[r], n * 16 + 16)
                    step(dve.tensor_copy(srcf[:, :], idx[r][:, :]))
                    step(dve.tensor_scalar(contc[:, :], cont[:, bass.ds(j * T, T)], 1.0, None, ALU.mult))
                    dve.wait_ge(s_bt, j + 1)
                    step(dve.scalar_tensor_tensor(BT[:, :, 0], F[:, :, T - 1], contc[:, 0:1],
                                                  BT[:, :, 0], ALU.mult, ALU.add))
                    flat = lambda ap: ap[:, :, :].rearrange("p f t -> p (f t)")
                    dve.tensor_tensor_scan(flat(F), flat(keep), flat(BT), 0.0, ALU.mult, ALU.add).then_inc(s_F, 1)
                    dve.wait_ge(s_g[r], n * (16 * T) + 16 * T)
                    dve.wait_ge(s_F, j + 2)
                    dve.tensor_tensor(H[:, :, :], G[r][:, :, :], F[:, :, :].rearrange("p f t -> p t f"),
                                      ALU.add).then_inc(s_H, 1)
                    for g, (t0, m) in enumerate(GROUPS):
                        b = g % 2
                        dve.wait_ge(s_B, j * NG + (g + 1))
                        step(dve.tensor_tensor(same[b][:, 0:m, :],
                                               bank[2 + b][:, 0:m * P].rearrange("p (t q) -> p t q", t=m),
                                               bc(srcf[:, t0:t0 + m], 2, [P, m, P]), ALU.is_equal))
                        step(dve.tensor_tensor(earlier[:, 0:m, :], same[b][:, 0:m, :],
                                               bc(below[:, :], 1, [P, m, P]), ALU.mult))
                        dve.tensor_reduce(dup[:, t0:t0 + m], earlier[:, 0:m, :], AX, ALU.add)
                        dve.wait_ge(s_sg, j * NG + (g + 1))
                        psI = bank[1][:, 0:m * 2 * D].rearrange("p (t f) -> p t f", t=m)
                        dve.tensor_tensor(msg[b][:, 0:m, 0:D], psI[:, :, 0:D], gate[:, 0:m, :],
                                          ALU.mult).then_inc(s_eq, 1)
                    dve.wait_ge(s_eq, j * NG + NG)
                    step(dve.tensor_scalar(dup[:, :], dup[:, :], 0.5, None, ALU.is_gt))
                    step(dve.tensor_scalar(to[:, :], srcf[:, :], -1.0, trash[:, 0:1], ALU.mult, ALU.add))
                    step(dve.tensor_tensor(to[:, :], to[:, :], dup[:, :], ALU.mult))
                    step(dve.tensor_tensor(to[:, :], to[:, :], srcf[:, :], ALU.add))
                    if since(j, RING):
                        for a in range(ACCS):
                            dve.wait_ge(acc_landed[a], (j - (RING - 1)) * (16 * T // ACCS) + 16)
                    dve.tensor_copy(idxs[r][:, :], to[:, :]).then_inc(s_to, 1)
                    step.end_chunk()
                chunk_loop(dve, body)

        w0.close()

        def store_out():
            with phase() as c:
                s_out = sem("out_stored")
                block = c.enter_context(nc.Block())

                @block.sync
                def _(sp):
                    xv = x_sb[:, :, :].rearrange("p k f -> p (k f)")
                    rows = lambda a, b: out[a * K:b * K, :].rearrange("(p k) f -> p (k f)", k=K)
                    for a, b in ((0, 96), (96, 126), (126, 127)):
                        sp.dma_start(rows(a, b), xv[a:b, :]).then_inc(s_out, 16)
                    rest = N - 127 * K
                    sp.dma_start(out[127 * K:N, :].rearrange("(p k) f -> p (k f)", k=rest),
                                 xv[127:128, 0:rest * D]).then_inc(s_out, 16)
                    sp.wait_ge(s_out, 64)


        def segments(tag, kind, table, idx_src, head, wrow, fin):
            width = {"attn": ROW + D, "gat": ROW, "rel": D}[kind]
            chans = D if kind == "rel" else D + 1
            with phase() as c:
                idx = [sb(c, f"{tag}_idx{r}", [P, T], I32) for r in range(RING)]
                G = [sb(c, f"{tag}_G{r}", [P, T, width]) for r in range(RING)]
                rows = [sb(c, f"{tag}_rows{r}", [P, T, ROW]) for r in range(RING)]
                contc = sb(c, f"{tag}_contc", [P, T])
                reset = sb(c, f"{tag}_reset", [P, T])
                logit = sb(c, f"{tag}_logit", [P, T])
                top = sb(c, f"{tag}_top", [P, T + 1])
                arg = sb(c, f"{tag}_arg", [P, 2, T])
                wd = sb(c, f"{tag}_wd", [P, 2, T])
                decay = sb(c, f"{tag}_decay", [P, chans, T])
                V = sb(c, f"{tag}_V", [P, chans, T])
                O = sb(c, f"{tag}_O", [P, chans, T])
                if kind == "attn":
                    Br = [sb(c, f"{tag}_Br{r}", [P, T, D]) for r in range(RING)]
                    keep = sb(c, f"{tag}_keep", [P, D, T])
                    BT = sb(c, f"{tag}_BT", [P, D, T])
                    F = sb(c, f"{tag}_F", [P, D, T])
                    H = sb(c, f"{tag}_H", [P, T, D])
                if kind == "gat":
                    adst = sb(c, f"{tag}_adst", [P, L])
                if kind == "rel":
                    norm = [sb(c, f"{tag}_norm{r}", [P, T]) for r in range(RING)]
                s_idx = [sem(f"{tag}_idx_loaded{r}") for r in range(RING)]
                s_g = [pool_dma_sem(f"{tag}_gathered{r}") for r in range(RING)]
                s_st = [sem(f"{tag}_rows_stored{r}") for r in range(RING)]
                s_br = [sem(f"{tag}_first_rows{r}") for r in range(RING)]
                (s_used, s_turn, s_F, s_H, s_tanh, s_arg, s_wd, s_dc, s_O, s_rows, s_ini, s_ad) = (
                    sem(f"{tag}_{n}") for n in (
                        "rows_used", "first_rows_turned", "filled", "added", "tanh_done", "args_done",
                        "weights_done", "decay_spread", "summed", "rows_made", "started", "adst_loaded"))
                block = c.enter_context(nc.Block())
                first_v = firstrows_d.rearrange("(p l) f -> p (l f)", p=P)
                state_v = state_d.rearrange("(p l) f -> p (l f)", p=P)
                norm_v = ew.rearrange("(p l) f -> p (l f)", p=P)
                flat = lambda ap: ap[:, :, :].rearrange("p f t -> p (f t)")

                @block.sync
                def _(sp):
                    if kind == "gat":
                        sp.dma_start(adst[:, :], firstad_d.rearrange("(p l) f -> p (l f)", p=P)).then_inc(s_ad, 16)

                    def body(j, r, n):
                        if since(j, RING):
                            sp.wait_ge(s_used, j - (RING - 1))
                        sp.dma_start(idx[r][:, :], idx_src[:, bass.ds(j * T, T)]).then_inc(s_idx[r], 16)
                        if kind == "rel":
                            sp.dma_start(norm[r][:, :], norm_v[:, bass.ds(j * T, T)]).then_inc(s_br[r], 16)
                        if kind == "attn":
                            if since(j, RING):
                                sp.wait_ge(s_turn, j - (RING - 1))
                            sp.dma_start(Br[r][:, :, :].rearrange("p t f -> p (t f)"),
                                         first_v[:, bass.ds(j * (T * D), T * D)]).then_inc(s_br[r], 16)
                    chunk_loop(sp, body)

                @block.gpsimd
                def _(pool):
                    def body(j, r, n):
                        hold(pool, s_idx[r], n * 16 + 16)
                        if since(j, RING):
                            hold(pool, s_used, j - (RING - 1))
                        for t in range(T):
                            pool.indirect_dma_start(
                                out=G[r][:, t, :], out_offset=None, in_=table,
                                in_offset=bass.IndirectOffsetOnAxis(ap=idx[r][:, t:t + 1], axis=0))\
                                .then_inc(s_g[r], 16)
                    chunk_loop(pool, body)

                @block.scalar
                def _(act):
                    act.wait_ge(s_ini, 1)

                    def body(j, r, n):
                        if kind == "attn":
                            act.wait_ge(s_br[r], n * 16 + 16)
                            if since(j, 1):
                                hold(act, s_F, j)
                            act.activation(BT[:, :, :].rearrange("p f t -> p t f"), Br[r][:, :, :], ACT.Copy)
                            act.activation(keep[:, :, 1:T],
                                           bc(cont[:, bass.ds(j * T + 1, T - 1)], 1, [P, D, T - 1]),
                                           ACT.Copy).then_inc(s_turn, 1)
                            act.wait_ge(s_H, j + 1)
                            act.activation(H[:, :, :], H[:, :, :], ACT.Tanh).then_inc(s_tanh, 1)
                        act.wait_ge(s_arg, j + 1)
                        if kind != "rel":
                            act.activation(wd[:, :, :], arg[:, :, :], ACT.Exp).then_inc(s_wd, 1)
                            act.wait_ge(s_wd, j + 1)
                        act.activation(decay[:, :, 1:T],
                                       bc(wd[:, 0, 1:T], 1, [P, chans, T - 1]), ACT.Copy).then_inc(s_dc, 1)
                        if since(j, RING):
                            act.wait_ge(s_st[r], n * 16)
                        act.wait_ge(s_O, j + 1)
                        act.activation(rows[r][:, :, 0:chans].rearrange("p t f -> p f t"), O[:, :, :], ACT.Copy)\
                            .then_inc(s_rows, 1)
                        if kind != "rel":
                            act.activation(rows[r][:, :, D + 1], top[:, 1:T + 1], ACT.Copy).then_inc(s_rows, 1)
                        act.wait_ge(s_rows, (j + 1) * (1 if kind == "rel" else 2))
                        act.dma_start(state_v[:, bass.ds(j * (T * ROW), T * ROW)],
                                      rows[r][:, :, :].rearrange("p t f -> p (t f)")).then_inc(s_st[r], 16)
                    chunk_loop(act, body)
                    for r in range(RING):
                        act.wait_ge(s_st[r], 16 * len(range(r, CH, RING)))

                @block.vector
                def _(dve):
                    step = Steps(dve, sem(f"order_{tag}"))
                    step(dve.memset(O[:, :, :], 0.0))
                    step(dve.memset(top[:, :], -BIG))
                    step(dve.memset(decay[:, :, :], 0.0))
                    if kind == "rel":
                        for r in range(RING):
                            step(dve.memset(rows[r][:, :, :], 0.0))
                    if kind == "attn":
                        step(dve.memset(F[:, :, :], 0.0))
                        step(dve.memset(keep[:, :, :], 0.0))
                        step(dve.tensor_copy(F[:, :, T - 1], head[:, :]))
                    if kind == "gat":
                        dve.wait_ge(s_ad, 16)
                        step(dve.tensor_tensor_scan(adst[:, :], cont[:, :], adst[:, :], head[:, 0:1],
                                                    ALU.mult, ALU.add))
                    dve.sem_inc(s_ini, 1)

                    def body(j, r, n):
                        step.chunk(j, {"attn": 11, "gat": 10, "rel": 3}[kind])
                        step(dve.tensor_scalar(contc[:, :], cont[:, bass.ds(j * T, T)], 1.0, None, ALU.mult))
                        if kind == "attn":
                            dve.wait_ge(s_turn, j + 1)
                            step(dve.scalar_tensor_tensor(BT[:, :, 0], F[:, :, T - 1], contc[:, 0:1],
                                                          BT[:, :, 0], ALU.mult, ALU.add))
                            dve.tensor_tensor_scan(flat(F), flat(keep), flat(BT), 0.0, ALU.mult, ALU.add)\
                                .then_inc(s_F, 1)
                            dve.wait_ge(s_F, j + 1)
                        dve.wait_ge(s_g[r], n * (16 * T) + 16 * T)
                        if kind == "attn":
                            dve.tensor_tensor(H[:, :, :], G[r][:, :, ROW:ROW + D],
                                              F[:, :, :].rearrange("p f t -> p t f"), ALU.add).then_inc(s_H, 1)
                            dve.wait_ge(s_tanh, j + 1)
                            step(dve.tensor_tensor(H[:, :, :], H[:, :, :], bc(wrow[:, :], 1, [P, T, D]), ALU.mult))
                            step(dve.tensor_reduce(logit[:, :], H[:, :, :], AX, ALU.add))
                        if kind == "gat":
                            step(dve.tensor_tensor(logit[:, :], adst[:, bass.ds(j * T, T)], G[r][:, :, D + 1],
                                                   ALU.add))
                            step(dve.scalar_tensor_tensor(logit[:, :], logit[:, :], NEG_SLOPE, logit[:, :],
                                                          ALU.mult, ALU.max))
                        if kind == "rel":
                            dve.tensor_copy(wd[:, 0, :], contc[:, :]).then_inc(s_arg, 1)
                            dve.wait_ge(s_br[r], n * 16 + 16)
                            weight = norm[r][:, :]
                        else:
                            if since(j, 1):
                                dve.wait_ge(s_rows, j * 2)
                            step(dve.tensor_scalar(reset[:, :], contc[:, :], 1.0, BIG, ALU.subtract, ALU.mult))
                            step(dve.tensor_copy(top[:, 0:1], top[:, T:T + 1]))
                            step(dve.tensor_tensor_scan(top[:, 1:T + 1], reset[:, :], logit[:, :], top[:, 0:1],
                                                        ALU.add, ALU.max))
                            step(dve.tensor_tensor(arg[:, 0, :], top[:, 0:T], reset[:, :], ALU.add))
                            step(dve.tensor_tensor(arg[:, 0, :], arg[:, 0, :], top[:, 1:T + 1], ALU.subtract))
                            dve.tensor_tensor(arg[:, 1, :], logit[:, :], top[:, 1:T + 1], ALU.subtract)\
                                .then_inc(s_arg, 1)
                            dve.wait_ge(s_wd, j + 1)
                            weight = wd[:, 1, :]
                        step(dve.tensor_tensor(V[:, :, :].rearrange("p f t -> p t f"), G[r][:, :, 0:chans],
                                               bc(weight, 2, [P, T, chans]), ALU.mult))
                        if kind == "rel":
                            dve.wait_ge(s_dc, j + 1)
                        step(dve.scalar_tensor_tensor(V[:, :, 0], O[:, :, T - 1], wd[:, 0, 0:1], V[:, :, 0],
                                                      ALU.mult, ALU.add))
                        dve.sem_inc(s_used, 1)
                        dve.wait_ge(s_dc, j + 1)
                        if kind == "rel" and since(j, 1):
                            dve.wait_ge(s_rows, j)
                        dve.tensor_tensor_scan(flat(O), flat(decay), flat(V), 0.0, ALU.mult, ALU.add)\
                            .then_inc(s_O, 1)
                        dve.wait_ge(s_O, j + 1)
                        step.end_chunk()
                    chunk_loop(dve, body)
                    step.end_loop(CH)
                    step(dve.memset(fin[:, :], 0.0))
                    step(dve.tensor_copy(fin[:, 0:chans], O[:, :, T - 1]))
                    if kind != "rel":
                        step(dve.tensor_copy(fin[:, D + 1:ROW], top[:, T:T + 1]))

        def hand_on(tag, fin):
            with phase() as c:
                t1 = sb(c, f"{tag}_t1", [P, P])
                ex = sb(c, f"{tag}_ex", [P, P])
                exT = sb(c, f"{tag}_exT", [P, P])
                tops = sb(c, f"{tag}_tops", [P, 2])
                ab = sb(c, f"{tag}_ab", [P, 2])
                U = sb(c, f"{tag}_U", [P, ROW])
                s_row, s_d, s_ex, s_m, s_t, s_c, s_in, s_ab, s_eab, s_new = (
                    sem(f"{tag}_{n}") for n in (
                        "tops_spread", "tops_off", "exps", "masked", "turned", "turn_copied", "handed",
                        "offsets", "factors", "merged"))
                s_u, s_fix = (pool_dma_sem(f"{tag}_{n}") for n in ("last_rows", "fixed"))
                block = c.enter_context(nc.Block())

                @block.tensor
                def _(pe):
                    pe.matmul(bank[0][:, 0:P], lhsT=fin[:, D + 1:ROW].to_broadcast([P, P]), rhs=ident[:, :],
                              start=True, stop=True).then_inc(s_row, 1)
                    pe.wait_ge(s_m, 1)
                    pe.transpose(bank[1][:, 0:P], ex[:, :], ident[:, :]).then_inc(s_t, 1)
                    pe.wait_ge(s_c, 1)
                    pe.matmul(bank[2][:, 0:D + 1], lhsT=exT[:, :], rhs=fin[:, 0:D + 1],
                              start=True, stop=True).then_inc(s_in, 1)

                @block.scalar
                def _(act):
                    act.wait_ge(s_d, 1)
                    act.activation(ex[:, :], t1[:, :], ACT.Exp).then_inc(s_ex, 1)
                    act.wait_ge(s_ab, 1)
                    act.activation(ab[:, :], ab[:, :], ACT.Exp).then_inc(s_eab, 1)

                @block.gpsimd
                def _(pool):
                    pool.indirect_dma_start(out=U[:, :], out_offset=None, in_=state_d,
                                            in_offset=bass.IndirectOffsetOnAxis(ap=lastq_i[:, 0:1], axis=0))\
                        .then_inc(s_u, 16)
                    pool.wait_ge(s_new, 1)
                    pool.indirect_dma_start(out=state_d,
                                            out_offset=bass.IndirectOffsetOnAxis(ap=fix_i[:, 0:1], axis=0),
                                            in_=U[:, :], in_offset=None,
                                            bounds_check=E - 1, oob_is_err=False).then_inc(s_fix, 16)
                    pool.wait_ge(s_fix, 16)

                @block.vector
                def _(dve):
                    step = Steps(dve, sem(f"order_{tag}"))
                    step(dve.tensor_scalar(t1[:, :], carryT[:, :], 1.0, BIG, ALU.subtract, ALU.mult))
                    dve.wait_ge(s_row, 1)
                    step(dve.tensor_tensor(t1[:, :], t1[:, :], bank[0][:, 0:P], ALU.add))
                    step(dve.tensor_reduce(tops[:, 0:1], t1[:, :], AX, ALU.max))
                    dve.tensor_scalar(t1[:, :], t1[:, :], tops[:, 0:1], None, ALU.subtract).then_inc(s_d, 1)
                    dve.wait_ge(s_ex, 1)
                    dve.tensor_tensor(ex[:, :], ex[:, :], carryT[:, :], ALU.mult).then_inc(s_m, 1)
                    dve.wait_ge(s_t, 1)
                    dve.tensor_copy(exT[:, :], bank[1][:, 0:P]).then_inc(s_c, 1)
                    dve.wait_ge(s_u, 16)
                    step(dve.tensor_tensor(tops[:, 1:2], tops[:, 0:1], U[:, D + 1:ROW], ALU.max))
                    step(dve.tensor_tensor(ab[:, 0:1], tops[:, 0:1], tops[:, 1:2], ALU.subtract))
                    dve.tensor_tensor(ab[:, 1:2], U[:, D + 1:ROW], tops[:, 1:2], ALU.subtract).then_inc(s_ab, 1)
                    dve.wait_ge(s_eab, 1)
                    step(dve.tensor_scalar(U[:, 0:D + 1], U[:, 0:D + 1], ab[:, 1:2], None, ALU.mult))
                    dve.wait_ge(s_in, 1)
                    step(dve.scalar_tensor_tensor(U[:, 0:D + 1], bank[2][:, 0:D + 1], ab[:, 0:1], U[:, 0:D + 1],
                                                  ALU.mult, ALU.add))
                    dve.tensor_copy(U[:, D + 1:ROW], tops[:, 1:2]).then_inc(s_new, 1)

        with phase() as w:
            w_attn = sb(w, "w_attn", [D, 2 * D])
            w_raw = sb(w, "w_raw", [D, 2 * D])
            bias1 = sb(w, "bias1", [P, 2 * D])
            wout = sb(w, "wout", [P, D])
            head1 = sb(w, "head1", [P, D])
            fin1 = sb(w, "fin1", [P, ROW])
            with phase() as c:
                s_w, s_t = sem("l1w_loaded"), sem("l1w_turned")
                block = c.enter_context(nc.Block())

                @block.sync
                def _(sp):
                    sp.dma_start(w_raw[:, :], W["L1_gnn_W_attn"]).then_inc(s_w, 16)
                    sp.dma_start(bias1[:, D:2 * D], bc(W["L1_gnn_b_attn"], 0, [P, D])).then_inc(s_w, 16)
                    sp.dma_start(wout[:, :], bc(W["L1_gnn_w_out"], 0, [P, D])).then_inc(s_w, 16)

                @block.tensor
                def _(pe):
                    pe.wait_ge(s_w, 48)
                    pe.transpose(bank[0][0:D, 0:D], w_raw[:, 0:D], ident[0:D, 0:D])
                    pe.transpose(bank[0][0:D, D:2 * D], w_raw[:, D:2 * D], ident[0:D, 0:D]).then_inc(s_t, 1)

                @block.vector
                def _(dve):
                    dve.memset(bias1[:, 0:D], 0.0)
                    dve.wait_ge(s_t, 1)
                    dve.tensor_copy(w_attn[:, :], bank[0][0:D, 0:2 * D])
            with phase() as c:
                tab = sb(c, "tab1", [P, K, ROW + 2 * D])
                A = [sb(c, f"A{b}", [P, ACCS, PART, D + 1]) for b in range(2)]
                cnt = sb(c, "edges_of", [P, PART])
                s_acc = [sem(f"acc_loaded{b}") for b in range(2)]

                def load(sp, q):
                    k0, k1 = PARTS[q]
                    for a in range(ACCS):
                        sp.dma_start(A[q % 2][:, a, 0:k1 - k0, :],
                                     acc_d[a][0:NP, :].rearrange("(p k) f -> p k f", k=K)[:, k0:k1, :])\
                            .then_inc(s_acc[q % 2], 16)

                def update(dve, step, q, k0, k1):
                    n, B = k1 - k0, A[q % 2]
                    dve.wait_ge(s_acc[q % 2], 16 * ACCS * (q // 2 + 1))
                    for a in range(1, ACCS):
                        step(dve.tensor_tensor(B[:, 0, 0:n, :], B[:, 0, 0:n, :], B[:, a, 0:n, :], ALU.add))
                    step(dve.tensor_scalar(cnt[:, 0:n], B[:, 0, 0:n, D], 1.0, None, ALU.max))
                    step(dve.reciprocal(cnt[:, 0:n], cnt[:, 0:n]))
                    step(dve.tensor_tensor(B[:, 0, 0:n, 0:D], B[:, 0, 0:n, 0:D], bc(cnt[:, 0:n], 2, [P, n, D]),
                                           ALU.mult))
                    step(dve.tensor_tensor(x_sb[:, k0:k1, :], x_sb[:, k0:k1, :], B[:, 0, 0:n, 0:D], ALU.add))

                def extra(dve, step, k0, k1):
                    step(dve.memset(tab[:, k0:k1, D:ROW], 1.0))
                    step(dve.tensor_copy(tab[:, k0:k1, 0:D], x_sb[:, k0:k1, :]))

                node_block("n0", load=load, update=update, norm=True, proj={
                    "of": (x_sb, w_attn[:, :], bias1[:, :], 2 * D, tab, ROW), "extra": extra,
                    "stores": [(tabB_d, ROW + D, ROW + 2 * D), (tabG_d, 0, ROW + D)],
                    "scatter": (firstrows_d, lambda k: tab[:, k, ROW + D:ROW + 2 * D]), "head": (head1, tabB_d)})
            segments("e1", "attn", tabG_d, src_c, head1, wout, fin1)
            hand_on("f1", fin1)

        with phase() as w:
            tabs = [sb(w, f"tab_c{i}", [P, K, ROW]) for i in (1, 2)]
            ads = [sb(w, f"ad_c{i}", [P, K]) for i in (1, 2)]
            heads = [sb(w, f"head_c{i}", [P, 1]) for i in (1, 2)]
            fin2 = sb(w, "fin_c", [P, ROW])
            zero_row = sb(w, "zero_row", [P, D])
            w2c = [sb(w, f"w2c{i}", [D, D]) for i in range(2)]
            rowsw = {n: sb(w, f"row_{n}", [P, D]) for n in ("as1", "ad1", "b1", "as2", "ad2", "b2", "bn_gamma",
                                                             "bn_beta", "bn_mean", "bn_var")}
            prod = sb(w, "prod", [P, HALF, D])
            with phase() as c:
                s_w, s_s = sem("l2w_loaded"), sem("l2w_sqrt")
                s_v = sem("l2w_var")
                block = c.enter_context(nc.Block())

                @block.sync
                def _(sp):
                    for i in range(2):
                        sp.dma_start(w2c[i][:, :], W[f"L2_gnn_W{i + 1}"]).then_inc(s_w, 16)
                    for n, t in rowsw.items():
                        sp.dma_start(t[:, :], bc(W[f"L2_gnn_{n}"], 0, [P, D])).then_inc(s_w, 16)

                @block.scalar
                def _(act):
                    act.wait_ge(s_v, 1)
                    act.activation(rowsw["bn_var"][:, :], rowsw["bn_var"][:, :], ACT.Sqrt).then_inc(s_s, 1)

                @block.vector
                def _(dve):
                    step = Steps(dve, sem("order_l2w"))
                    g, be, mu, va = (rowsw[f"bn_{n}"][:, :] for n in ("gamma", "beta", "mean", "var"))
                    dve.memset(zero_row[:, :], 0.0)
                    dve.wait_ge(s_w, 16 * 12)
                    dve.tensor_scalar(va, va, BN_EPS, None, ALU.add).then_inc(s_v, 1)
                    dve.wait_ge(s_s, 1)
                    step(dve.reciprocal(va, va))
                    step(dve.tensor_tensor(g, g, va, ALU.mult))
                    step(dve.tensor_tensor(mu, mu, g, ALU.mult))
                    step(dve.tensor_tensor(be, be, mu, ALU.subtract))

            def conv_tables(conv, h_in):
                tab, ad = tabs[conv - 1], ads[conv - 1]

                def extra(dve, step, k0, k1):
                    n = k1 - k0
                    step(dve.memset(tab[:, k0:k1, D], 1.0))
                    for name, dest in ((f"ad{conv}", ad[:, k0:k1]), (f"as{conv}", tab[:, k0:k1, D + 1])):
                        step(dve.tensor_tensor(prod[:, 0:n, :], tab[:, k0:k1, 0:D],
                                               bc(rowsw[name][:, :], 1, [P, n, D]), ALU.mult))
                        step(dve.tensor_reduce(dest, prod[:, 0:n, :], AX, ALU.add))

                return {"of": (h_in, w2c[conv - 1][:, :], zero_row[:, :], D, tab, 0), "extra": extra,
                        "stores": [(tabS_d, None, ad), (tabH_d, 0, ROW)],
                        "scatter": (firstad_d, lambda k: ad[:, k:k + 1]), "head": (heads[conv - 1], tabS_d)}

            with phase() as c:
                S = sb(c, "S1", [P, K, ROW])
                z = sb(c, "z1", [P, PART, D])
                den = sb(c, "den1", [P, PART])

                def update(dve, step, q, k0, k1):
                    n, ne = k1 - k0, nonempty[:, k0:k1]
                    d = den[:, 0:n]
                    step(dve.tensor_tensor(d, S[:, k0:k1, D], ne, ALU.mult))
                    step(dve.scalar_tensor_tensor(d, d, 0.0, d, ALU.is_equal, ALU.add))
                    step(dve.reciprocal(d, d))
                    step(dve.tensor_tensor(d, d, ne, ALU.mult))
                    step(dve.tensor_tensor(z[:, 0:n, :], S[:, k0:k1, 0:D], bc(d, 2, [P, n, D]), ALU.mult))
                    step(dve.tensor_tensor(x_sb[:, k0:k1, :], x_sb[:, k0:k1, :], z[:, 0:n, :], ALU.add))

                node_block("n1", collect=S, update=update, norm=True, proj=conv_tables(1, x_sb))

            for conv in (1, 2):
                tab, ad = tabs[conv - 1], ads[conv - 1]
                tg = f"c{conv}"
                segments(f"{tg}e", "gat", tabH_d, src_c, heads[conv - 1], None, fin2)
                hand_on(f"{tg}f", fin2)
                with phase() as c:
                    S = sb(c, f"{tg}_S", [P, K, ROW])
                    m = sb(c, f"{tg}_mx", [P, PART])
                    own = sb(c, f"{tg}_own", [P, PART])
                    top = sb(c, f"{tg}_topn", [P, PART])
                    ab = sb(c, f"{tg}_abn", [P, 2, PART])
                    z = sb(c, f"{tg}_z", [P, PART, D])
                    h_mid = sb(c, f"{tg}_h_mid", [P, K, D]) if conv == 1 else None
                    s_ab, s_eab = sem(f"{tg}n_offsets"), sem(f"{tg}n_factors")

                    def act_update(act, q, k0, k1):
                        act.wait_ge(s_ab, q + 1)
                        act.activation(ab[:, :, 0:k1 - k0], ab[:, :, 0:k1 - k0], ACT.Exp).then_inc(s_eab, 1)

                    def update(dve, step, q, k0, k1):
                        n, ne = k1 - k0, nonempty[:, k0:k1]
                        o, t, mm, a, b = own[:, 0:n], top[:, 0:n], m[:, 0:n], ab[:, 0, 0:n], ab[:, 1, 0:n]
                        wide, zz = [P, n, D], z[:, 0:n, :]
                        tq, Sq = tab[:, k0:k1, 0:D], S[:, k0:k1, 0:D]
                        step(dve.tensor_tensor(o, tab[:, k0:k1, D + 1], ad[:, k0:k1], ALU.add))
                        step(dve.scalar_tensor_tensor(o, o, NEG_SLOPE, o, ALU.mult, ALU.max))
                        step(dve.tensor_scalar(mm, ne, 1.0, BIG, ALU.subtract, ALU.mult))
                        step(dve.tensor_tensor(t, S[:, k0:k1, D + 1], ne, ALU.mult))
                        step(dve.tensor_tensor(mm, mm, t, ALU.add))
                        step(dve.tensor_tensor(t, mm, o, ALU.max))
                        step(dve.tensor_tensor(a, o, t, ALU.subtract))
                        dve.tensor_tensor(b, mm, t, ALU.subtract).then_inc(s_ab, 1)
                        dve.wait_ge(s_eab, q + 1)
                        step(dve.tensor_tensor(b, b, ne, ALU.mult))
                        step(dve.tensor_tensor(mm, S[:, k0:k1, D], b, ALU.mult))
                        step(dve.tensor_tensor(mm, mm, a, ALU.add))
                        step(dve.tensor_scalar(mm, mm, 1e-16, None, ALU.add))
                        step(dve.reciprocal(mm, mm))
                        step(dve.tensor_tensor(ab[:, :, 0:n], ab[:, :, 0:n], bc(mm, 1, [P, 2, n]), ALU.mult))
                        step(dve.tensor_tensor(zz, Sq, bc(b, 2, wide), ALU.mult))
                        step(dve.tensor_tensor(tq, tq, bc(a, 2, wide), ALU.mult))
                        step(dve.tensor_tensor(zz, zz, tq, ALU.add))
                        step(dve.tensor_tensor(zz, zz, bc(rowsw[f"b{conv}"][:, :], 1, wide), ALU.add))
                        if conv == 1:
                            hq = h_mid[:, k0:k1, :]
                            step(dve.scalar_tensor_tensor(hq, zz, 0.0, bc(rowsw["bn_gamma"][:, :], 1, wide),
                                                          ALU.max, ALU.mult))
                            step(dve.tensor_tensor(hq, hq, bc(rowsw["bn_beta"][:, :], 1, wide), ALU.add))
                        else:
                            xq = x_sb[:, k0:k1, :]
                            step(dve.scalar_tensor_tensor(xq, zz, 0.0, xq, ALU.max, ALU.add))

                    node_block(f"{tg}n", collect=S, update=update, act_update=act_update, norm=(conv == 2),
                               proj=conv_tables(2, h_mid) if conv == 1 else None)

        with phase() as w:
            w_hh = sb(w, "w_hh", [P, R * D], BF16)
            w_mm = sb(w, "w_mm", [P, R * D], BF16)
            w_lh = sb(w, "w_lh", [P, R * D], BF16)
            identb = sb(w, "identb", [P, P], BF16)
            w_res = sb(w, "w_res", [D, D])
            rows3 = {n: sb(w, f"row_{n}", [P, D]) for n in ("bias", "res_b", "gamma", "beta")}
            fin3 = sb(w, "fin3", [P, ROW])
            NB = R * D // 512
            with phase() as c:
                comp = sb(c, "comp", [R, R])
                compT = sb(c, "compT", [R, R])
                basis = sb(c, "basis", [R, D * D])
                wr = sb(c, "wr", [R, D * D])
                res_raw = sb(c, "res_raw", [D, D])
                w3 = sb(c, "w3", [P, R * D])
                s_hi = sem("l3w_high_made")
                s_w, s_t, s_tc, s_mm, s_wr, s_wrd, s_w3 = (sem(f"l3w_{n}") for n in (
                    "loaded", "turned", "copied", "mixed", "mix_copied", "mix_stored", "mix_loaded"))
                block = c.enter_context(nc.Block())

                @block.sync
                def _(sp):
                    sp.dma_start(comp[:, :], W["L3_gnn_comp"]).then_inc(s_w, 16)
                    sp.dma_start(basis[:, :], W["L3_gnn_basis"].rearrange("b i o -> b (i o)")).then_inc(s_w, 16)
                    sp.dma_start(res_raw[:, :], W["L3_gnn_res_w"]).then_inc(s_w, 16)
                    for n, t in rows3.items():
                        sp.dma_start(t[:, :], bc(W[f"L3_gnn_{n}"], 0, [P, D])).then_inc(s_w, 16)
                    sp.wait_ge(s_w, 16 * 7)
                    sp.wait_ge(s_wr, NB)
                    sp.dma_start(wr_d, wr[:, :]).then_inc(s_wrd, 16)
                    sp.wait_ge(s_wrd, 16)
                    sp.dma_start(w3[0:D, :].rearrange("i (r o) -> i r o", o=D),
                                 wr_d.rearrange("r (i o) -> i r o", o=D)).then_inc(s_w3, 16)

                @block.scalar
                def _(act):
                    act.wait_ge(s_wrd, 16)
                    act.dma_start(w3[D:P, :].rearrange("i (r o) -> i r o", o=D),
                                  wr_d.rearrange("r (i o) -> i r o", o=D)).then_inc(s_w3, 16)
                    act.wait_ge(s_hi, 1)
                    act.activation(w_lh[D:P, :], w_hh[D:P, :], ACT.Copy)

                @block.tensor
                def _(pe):
                    pe.wait_ge(s_w, 16 * 7)
                    pe.transpose(bank[0][0:R, 0:R], comp[:, :], ident[0:R, 0:R])
                    pe.transpose(bank[0][0:D, D:2 * D], res_raw[:, :], ident[0:D, 0:D]).then_inc(s_t, 1)
                    pe.wait_ge(s_tc, 2)
                    for q in range(NB):
                        pe.matmul(bank[q][0:R, :], lhsT=compT[:, :], rhs=basis[:, q * 512:(q + 1) * 512],
                                  start=True, stop=True).then_inc(s_mm, 1)

                @block.vector
                def _(dve):
                    dve.wait_ge(s_t, 1)
                    dve.tensor_copy(compT[:, :], bank[0][0:R, 0:R]).then_inc(s_tc, 1)
                    dve.tensor_copy(w_res[:, :], bank[0][0:D, D:2 * D]).then_inc(s_tc, 1)
                    for q in range(NB):
                        dve.wait_ge(s_mm, q + 1)
                        dve.tensor_copy(wr[:, q * 512:(q + 1) * 512], bank[q][0:R, :]).then_inc(s_wr, 1)
                    step = Steps(dve, s_hi)
                    dve.tensor_copy(identb[:, :], ident[:, :])
                    dve.wait_ge(s_w3, 32)
                    step(dve.tensor_copy(w_hh[:, :], w3[:, :]))
                    step(dve.tensor_tensor(w3[:, :], w3[:, :], w_hh[:, :], ALU.subtract))
                    step(dve.tensor_copy(w_mm[:, :], w3[:, :]))
                    step(dve.tensor_tensor(w3[0:D, :], w3[0:D, :], w_mm[0:D, :], ALU.subtract))
                    step(dve.tensor_copy(w_lh[0:D, :], w3[0:D, :]))

            with phase() as c:
                xc = sb(c, "l3_xc", [P, 2, 4, D], BF16)
                left = sb(c, "l3_left", [P, 2, D])
                xT = [sb(c, f"l3_xT{b}", [P, 4 * P], BF16) for b in range(2)]
                turned_x = [bank[h][:, 0:P].bitcast(BF16) for h in (0, 5)]
                yb = [sb(c, f"yb{b}", [P, R * D]) for b in range(4)]
                s_cut, s_t, s_lo, s_hi = (sem(f"l3t_{n}") for n in ("cut", "turned", "low_copied", "high_copied"))
                s_mm = [sem(f"l3t_multiplied{e}") for e in range(2)]
                s_ev = [sem(f"l3t_copied{e}") for e in range(2)]
                s_y = [sem(f"l3t_stored{b}") for b in range(4)]
                y_v = y_d.rearrange("(p q) f -> p (q f)", p=P)
                TRIPS = K // 2
                block = c.enter_context(nc.Block())

                def trips(eng, body):
                    for t in range(3):
                        body(t, t % 2, t // 2)
                    with eng.Fori(0, (TRIPS - 5) // 2) as i:
                        body(i * 2 + 3, 1, i + 1)
                        body(i * 2 + 4, 0, i + 2)
                    for t in range(TRIPS - 2, TRIPS):
                        body(t, t % 2, t // 2)

                @block.gpsimd
                def _(pool):
                    step = Steps(pool, sem("order_l3t"), apart=True)

                    def body(t, b, n):
                        if since(t, 1):
                            hold(pool, s_t, t)
                        high, middle, high2, low = (xc[:, :, i, :] for i in range(4))
                        all_left = left[:, :, :]
                        step.chunk(t, 5)
                        step(pool.tensor_copy(all_left, x_sb[:, bass.ds(t * 2, 2), :]))
                        step(pool.tensor_copy(high, all_left))
                        step(pool.tensor_tensor(all_left, all_left, high, ALU.subtract))
                        pool.tensor_copy(high2, high)
                        step(pool.tensor_copy(middle, all_left))
                        step(pool.tensor_tensor(all_left, all_left, middle, ALU.subtract))
                        pool.tensor_copy(low, all_left).then_inc(s_cut, 1)
                    trips(pool, body)

                @block.tensor
                def _(pe):
                    def turn(t):
                        hold(pe, s_cut, t + 1)
                        for i in range(4):
                            ins = pe.transpose(turned_x[i // 2][:, i % 2 * P:(i % 2 + 1) * P],
                                               xc[:, i // 2, 2 * (i % 2):2 * (i % 2) + 2, :], identb[:, :])
                        ins.then_inc(s_t, 1)

                    def body(t, b, n):
                        hold(pe, s_lo, t + 1)
                        hold(pe, s_hi, t + 1)
                        for m in range(2 * NB):
                            h, q, e = m // NB, m % NB, m % 2
                            if m == 4 and not (isinstance(t, int) and t == TRIPS - 1):
                                turn(t + 1)
                            if m >= 4 or since(t, 1):
                                hold(pe, s_ev[e], t * NB + (m // 2 - 1))
                            for i, (xpart, wpart) in enumerate(((0, w_hh), (0, w_mm), (1, w_lh))):
                                ins = pe.matmul(bank[1 + m % 4][:, :],
                                                lhsT=xT[b][:, (2 * h + xpart) * P:(2 * h + xpart + 1) * P],
                                                rhs=wpart[:, q * 512:(q + 1) * 512], start=(i == 0), stop=(i == 2))
                            ins.then_inc(s_mm[e], 1)
                    turn(0)
                    trips(pe, body)

                def copies(eng, e, t, b, n, turned, copy):
                    for m in range(e, 2 * NB, 2):
                        h, q = m // NB, m % NB
                        if q == e and since(t, 2):
                            hold(eng, s_y[2 * b + h], n * 16)
                        eng.wait_ge(s_mm[e], t * NB + (m // 2 + 1))
                        copy(yb[2 * b + h][:, q * 512:(q + 1) * 512], bank[1 + m % 4][:, :]).then_inc(s_ev[e], 1)
                        if m // 2 == 3 and not (isinstance(t, int) and t == TRIPS - 1):
                            turned(t + 1, 1 - b)

                @block.scalar
                def _(act):
                    def turned(t, b):
                        act.wait_ge(s_t, t + 1)
                        act.activation(xT[b][:, 0:2 * P], turned_x[0], ACT.Copy).then_inc(s_lo, 1)
                    turned(0, 0)
                    trips(act, lambda t, b, n: copies(act, 0, t, b, n, turned,
                                                   lambda o, a: act.activation(o, a, ACT.Copy)))

                @block.vector
                def _(dve):
                    def turned(t, b):
                        dve.wait_ge(s_t, t + 1)
                        dve.tensor_copy(xT[b][:, 2 * P:4 * P], turned_x[1]).then_inc(s_hi, 1)
                    turned(0, 0)
                    trips(dve, lambda t, b, n: copies(dve, 1, t, b, n, turned, lambda o, a: dve.tensor_copy(o, a)))

                @block.sync
                def _(sp):
                    def body(t, b, n):
                        for h in range(2):
                            for e in range(2):
                                sp.wait_ge(s_ev[e], t * NB + NB // 2 * (h + 1))
                            sp.dma_start(y_v[:, bass.ds(t * (2 * R * D) + h * R * D, R * D)], yb[2 * b + h][:, :])\
                                .then_inc(s_y[2 * b + h], 16)
                    trips(sp, body)
                    for b in range(4):
                        sp.wait_ge(s_y[b], 16 * len(range(b // 2, TRIPS, 2)))

            segments("e3", "rel", y_d, idx3_d, None, None, fin3)
            hand_on("f3", fin3)
            with phase() as c:
                S = sb(c, "S3", [P, K, ROW])
                res = sb(c, "res3", [P, K, D])
                sq = sb(c, "sq3", [P, K, D])
                m = sb(c, "m3", [P, K])
                part = sb(c, "part3", [P, D])
                sums = sb(c, "sums3", [P, len(PARTS), D])
                mean = sb(c, "mean3", [P, D])
                s_all = [pool_dma_sem(f"f3_collected{q}") for q in range(len(PARTS))]
                turn, copy, multiply, put, s_o = projection("l3p", c, x_sb, w_res[:, :], rows3["res_b"][:, :], D, res, 0)
                s_var, s_std, s_p, s_tot, s_bv, s_bs = (sem(f"n3_{n}") for n in (
                    "var", "std", "partial", "total", "batch_var", "batch_std"))
                block = c.enter_context(nc.Block())

                @block.gpsimd
                def _(pool):
                    for k in range(K):
                        pool.indirect_dma_start(out=S[:, k, :], out_offset=None, in_=state_d,
                                                in_offset=bass.IndirectOffsetOnAxis(ap=last_i[:, k:k + 1], axis=0))\
                            .then_inc(s_all[k // PART], 16)
                    for q, (k0, k1) in enumerate(PARTS):
                        pool.wait_ge(s_all[q], 16 * (k1 - k0))

                @block.tensor
                def _(pe):
                    turn(pe, 0)
                    for g in range(len(HALVES)):
                        if g + 1 < len(HALVES):
                            turn(pe, g + 1)
                        multiply(pe, g)
                    for v in range(2):
                        pe.wait_ge(s_p, v + 1)
                        pe.matmul(bank[v][:, 0:D], lhsT=ones[:, :], rhs=part[:, :], start=True, stop=True)\
                            .then_inc(s_tot, 1)

                @block.scalar
                def _(act):
                    for g in range(len(HALVES)):
                        copy(act, g)
                    act.wait_ge(s_bv, 1)
                    act.activation(mean[:, :], mean[:, :], ACT.Sqrt).then_inc(s_bs, 1)
                    layernorm(None, act, None, None, m, s_var, s_std, "act")

                @block.vector
                def _(dve):
                    step = Steps(dve, sem("order_n3"))
                    for g in range(len(HALVES)):
                        put(dve, step, g)
                        dve.sem_inc(s_o, 1)
                    y = sq[:, :, :]
                    pad = N - (P - 1) * K
                    over_nodes = lambda ap: ap.rearrange("p k f -> p f k")
                    for q, (k0, k1) in enumerate(PARTS):
                        yq, wide = sq[:, k0:k1, :], [P, k1 - k0, D]
                        dve.wait_ge(s_all[q], 16 * (k1 - k0))
                        step(dve.tensor_tensor(yq, S[:, k0:k1, 0:D], bc(nonempty[:, k0:k1], 2, wide), ALU.mult))
                        step(dve.tensor_tensor(yq, yq, bc(rows3["bias"][:, :], 1, wide), ALU.add))
                        step(dve.tensor_scalar(yq, yq, 0.0, None, ALU.max))
                        step(dve.scalar_tensor_tensor(yq, res[:, k0:k1, :], 0.0, yq, ALU.max, ALU.add))
                        if k1 > pad:
                            step(dve.tensor_tensor(yq, yq, bc(real[:, k0:k1], 2, wide), ALU.mult))
                        step(dve.tensor_reduce(sums[:, q, :], over_nodes(yq), AX, ALU.add))
                    dve.tensor_reduce(part[:, :], over_nodes(sums[:, :, :]), AX, ALU.add).then_inc(s_p, 1)
                    dve.wait_ge(s_tot, 1)
                    step(dve.tensor_scalar(mean[:, :], bank[0][:, 0:D], 1.0 / N, None, ALU.mult))
                    step(dve.tensor_tensor(y, y, bc(mean[:, :], 1, [P, K, D]), ALU.subtract))
                    step(dve.tensor_tensor(sq[:, pad:K, :], sq[:, pad:K, :],
                                           bc(real[:, pad:K], 2, [P, K - pad, D]), ALU.mult))
                    step(dve.tensor_tensor(res[:, :, :], y, y, ALU.mult))
                    dve.tensor_reduce(part[:, :], over_nodes(res[:, :, :]), AX, ALU.add).then_inc(s_p, 1)
                    dve.wait_ge(s_tot, 2)
                    dve.tensor_scalar(mean[:, :], bank[1][:, 0:D], 1.0 / N, BN_EPS, ALU.mult, ALU.add).then_inc(s_bv, 1)
                    dve.wait_ge(s_bs, 1)
                    step(dve.reciprocal(mean[:, :], mean[:, :]))
                    step(dve.tensor_tensor(mean[:, :], mean[:, :], rows3["gamma"][:, :], ALU.mult))
                    step(dve.tensor_tensor(y, y, bc(mean[:, :], 1, [P, K, D]), ALU.mult))
                    step(dve.tensor_tensor(y, y, bc(rows3["beta"][:, :], 1, [P, K, D]), ALU.add))
                    step(dve.tensor_tensor(x_sb[:, :, :], x_sb[:, :, :], y, ALU.add))
                    layernorm(dve, None, step, y, m, s_var, s_std, "dve")
        store_out()


_INS = ["x", "src", "dst", "edge_type_64", "edge_weight1"]
_WEIGHTS = ["L0_gnn_W1", "L0_gnn_b1", "L0_gnn_W2", "L0_gnn_b2", "L0_gnn_Wg", "L0_gnn_bg",
            "L1_gnn_W_attn", "L1_gnn_b_attn", "L1_gnn_w_out",
            "L2_gnn_W1", "L2_gnn_as1", "L2_gnn_ad1", "L2_gnn_b1", "L2_gnn_bn_gamma", "L2_gnn_bn_beta",
            "L2_gnn_bn_mean", "L2_gnn_bn_var", "L2_gnn_W2", "L2_gnn_as2", "L2_gnn_ad2", "L2_gnn_b2",
            "L3_gnn_basis", "L3_gnn_comp", "L3_gnn_bias", "L3_gnn_res_w", "L3_gnn_res_b",
            "L3_gnn_gamma", "L3_gnn_beta"]


def kernel(**inputs):
    import numpy as _np
    import concourse.bacc as _bacc
    from concourse import mybir as _mybir
    from concourse.bass_utils import run_bass_kernel_spmd as _run

    nc = _bacc.Bacc("TRN2", target_bir_lowering=False, num_devices=1)
    arrays, aps = {}, {}
    for name in _INS + _WEIGHTS:
        a = _np.ascontiguousarray(inputs[name])
        arrays[f"in_{name}"] = a
        aps[name] = nc.dram_tensor(f"in_{name}", a.shape, _mybir.dt.from_np(a.dtype), kind="ExternalInput").ap()
    out = nc.dram_tensor("out_0", (N, D), F32, kind="ExternalOutput").ap()
    program(nc, *(aps[n] for n in _INS), {n: aps[n] for n in _WEIGHTS}, out)
    r = _run(nc, [arrays], core_ids=[0])
    return r.results[0]["out_0"]
```
